# Optimizing a Trainium2 kernel written in Bass

```python
import numpy as np
import jax
import jax.numpy as jnp

def _softmax(x, axis=-1):
    return jax.nn.softmax(x, axis=axis)

def _gelu(x):
    return jax.nn.gelu(x, approximate=True)

def _silu(x):
    return jax.nn.silu(x)

def _sigmoid(x):
    return jax.nn.sigmoid(x)

def _layernorm(x, axis=-1, eps=1e-05):
    m = jnp.mean(x, axis=axis, keepdims=True)
    v = jnp.var(x, axis=axis, keepdims=True)
    return (x - m) / jnp.sqrt(v + eps)

def _scatter_add(tgt, idx, src, axis=0):
    return tgt.at[idx].add(src)

def _segment_sum(src, seg, n):
    return jax.ops.segment_sum(src, seg, n)
kernel_name = 'mk_xattn_ffn_d1_seqx_r2_a9c83a'

def setup_inputs(seed: int=0):
    np.random.seed(seed)
    _w = jnp.asarray

    def _rec_inputs():
        import jax
        import jax.numpy as jnp
        _rk = jax.random.key(seed)
        x = -7.109e-05 + 0.9999 * jax.random.normal(jax.random.fold_in(_rk, 1), (8, 224, 2048), jnp.float32)
        _lenS = 224 - jax.random.randint(jax.random.fold_in(_rk, 7), (8,), 0, max(1, 224 // 4) + 1, jnp.int32)
        _lenS2 = 750 - jax.random.randint(jax.random.fold_in(_rk, 8), (8,), 0, max(1, 750 // 4) + 1, jnp.int32)
        _ctx_4096P = jax.random.normal(jax.random.fold_in(_rk, 11), (8, 16, 2048), jnp.float32)
        _ctx_4096c = jax.random.dirichlet(jax.random.fold_in(_rk, 511), 0.3 * jnp.ones((16,), jnp.float32), (8, 750))
        _ctx_4096t = jnp.einsum('bsk,bkd->bsd', _ctx_4096c, _ctx_4096P)
        _ctx_4096t = _ctx_4096t * jax.lax.rsqrt(jnp.mean(jnp.square(_ctx_4096t)) + 1e-12) * 0.953939
        ctx_4096 = -0.00010331 + 0.999899 * (_ctx_4096t + 0.3 * jax.random.normal(jax.random.fold_in(_rk, 611), (8, 750, 2048), jnp.float32))
        return (x, ctx_4096)
    x, ctx_4096 = _rec_inputs()

    def _L0_xattn_setup():
        import jax, jax.numpy as jnp
        import numpy as np
        key = jax.random.key(seed)
        k1, k2 = jax.random.split(key)
        B, Lq, Lk, D = (16, 512, 1024, 2048)
        query = jax.random.normal(k1, (B, Lq, D), dtype=jnp.float32)
        key_t = jax.random.normal(k2, (B, Lk, D), dtype=jnp.float32)
        return {'query': query, 'key': key_t}
    _L0_xattn_all = _L0_xattn_setup()
    _L0_xattn_in = {k: v for k, v in _L0_xattn_all.items() if k in ()}
    del _L0_xattn_all

    def _L0_ffn_setup():
        import jax, jax.numpy as jnp
        import numpy as np
        TOP_K = 2
        SCALING = 32.0 / 64.0
        key = jax.random.key(seed)
        ks = jax.random.split(key, 6)
        Bsz, S, Din, Dout, R, E = (4, 1024, 2048, 2048, 64, 16)
        x = jax.random.normal(ks[0], (Bsz, S, Din), dtype=jnp.float32)
        base_w = jax.random.normal(ks[1], (Dout, Din), dtype=jnp.float32) * 0.02
        base_b = jax.random.normal(ks[2], (Dout,), dtype=jnp.float32) * 0.02
        A = jax.random.normal(ks[3], (R, Din), dtype=jnp.float32) * (1.0 / np.sqrt(Din))
        B = jax.random.normal(ks[4], (E, Dout, R), dtype=jnp.float32) * 0.02
        router_w = jax.random.normal(ks[5], (E, Din), dtype=jnp.float32) * 0.02
        return {'x': x, 'base_w': base_w, 'base_b': base_b, 'A': A, 'B': B, 'router_w': router_w}
    _L0_ffn_all = _L0_ffn_setup()
    _L0_ffn_in = {k: v for k, v in _L0_ffn_all.items() if k in ('base_w', 'base_b', 'A', 'B', 'router_w')}
    del _L0_ffn_all
    return {'x': x, 'ctx_4096': ctx_4096, 'L0_ffn_base_w': _L0_ffn_in['base_w'], 'L0_ffn_base_b': _L0_ffn_in['base_b'], 'L0_ffn_A': _L0_ffn_in['A'], 'L0_ffn_B': _L0_ffn_in['B'], 'L0_ffn_router_w': _L0_ffn_in['router_w']}

def reference(x, ctx_4096, L0_ffn_base_w, L0_ffn_base_b, L0_ffn_A, L0_ffn_B, L0_ffn_router_w):
    import jax
    import jax.numpy as jnp

    def _L0_xattn_ref(query, key):
        import jax, jax.numpy as jnp
        import numpy as np
        a = jnp.einsum('bqd,bkd->bqk', query, key)
        e = jax.nn.softmax(a, axis=-1)
        c = jnp.einsum('bqk,bkd->bqd', e, key)
        return c

    def _L0_ffn_ref(x, base_w, base_b, A, B, router_w):
        import jax, jax.numpy as jnp
        import numpy as np
        TOP_K = 2
        SCALING = 32.0 / 64.0
        base_out = jnp.einsum('bsi,oi->bso', x, base_w) + base_b
        res_hidden = jnp.einsum('bsi,ri->bsr', x, A)
        logits = jnp.einsum('bsi,ei->bse', x, router_w)
        probs = jax.nn.softmax(logits, axis=-1)
        topw, topi = jax.lax.top_k(probs, TOP_K)
        topw = topw / (jnp.sum(topw, axis=-1, keepdims=True) + 1e-06)
        num_experts = B.shape[0]
        combine = jnp.sum(jax.nn.one_hot(topi, num_experts, dtype=x.dtype) * topw[..., None], axis=-2)
        delta = jnp.einsum('bse,bsr,eor->bso', combine, res_hidden, B)
        return base_out + delta * SCALING
    x = x + _L0_xattn_ref(_layernorm(x, axis=-1), ctx_4096)
    x = x + _L0_ffn_ref(_layernorm(x, axis=-1), L0_ffn_base_w, L0_ffn_base_b, L0_ffn_A, L0_ffn_B, L0_ffn_router_w)
    return x

_drawn_inputs = setup_inputs


def setup_inputs(seed=0):
    import zlib

    import numpy as np

    out = dict(_drawn_inputs(seed))
    spreads = {}
    factors = {'L0_ffn_base_b': 5.508}
    for name, (base, spread) in spreads.items():
        noise = np.random.default_rng([zlib.crc32(name.encode()), seed]).standard_normal(out[name].shape)
        drawn = base * np.exp(spread * noise) if base else spread * noise
        out[name] = jnp.asarray(drawn.astype(out[name].dtype))
    for name, factor in factors.items():
        out[name] = (out[name] * factor).astype(out[name].dtype)
    return out
```

```python
from contextlib import ExitStack

import concourse.bass as bass
from concourse import mybir

ALU = mybir.AluOpType
ACT = mybir.ActivationFunctionType
AX = mybir.AxisListType
F32 = mybir.dt.float32
F32R = mybir.dt.float32r

P = 128
BANK = 512
EPS = 1e-5
TOP_EPS = 1e-6
SCALING = 0.5
STATS = 6


def as_f32(ap):
    return ap.bitcast(F32)


def at_least(eng, sem, value):
    if isinstance(value, int) and value <= 0:
        return
    eng.wait_ge(sem, value)


def build_identity(pool, ident, sem):
    pool.memset(ident[:, :], 0.0).then_inc(sem, 1)
    pool.wait_ge(sem, 1)
    pool.affine_select(out=ident[:, :], in_=ident[:, :], compare_op=ALU.not_equal, fill=1.0, base=0,
                       pattern=[[-1, P]], channel_multiplier=1).then_inc(sem, 1)


def attention_phase(nc, x, ctx, A, router, x2_d, xT_d, gT_d):
    NB, LQ, D = x.shape
    LK = ctx.shape[1]
    R, E = A.shape[0], router.shape[0]
    QT = LQ // 2
    NQ = 2
    KD = D // P
    NT = -(-LK // P)
    FULL = LK // P
    REST = LK - FULL * P
    CH = D // BANK
    RE = R + E
    G = R * E
    KG = G // P
    LOGITS = 16
    assert LQ == NQ * QT and D == CH * BANK and RE <= P and G % P == 0

    x_v = x.rearrange("b (q p) d -> b p q d", p=QT)
    x2_v = x2_d.rearrange("(b q p) d -> b p q d", q=NQ, p=QT)

    NX = KD // 4
    NG = KG // 4
    def group(name, n):
        return [(name, i) for i in range(n)]
    PRE = group("arT", 2) + group("qT", NX)
    FIRST = group("ctxT", KD) + group("eT", NQ) + group("qT", NX)
    MID = group("ctxT", KD) + group("x2T", NX) + [("hid", 0)] + group("eT", NQ) + [("hN", 0)] + group("gT", NG) + group("qT", NX)
    TAIL = group("x2T", NX) + [("hid", 0), ("hN", 0)] + group("gT", NG)
    BY_ACT = ("arT", "qT", "ctxT", "x2T", "eT")

    def count(jobs, stage_of, b, job, only=None):
        kept = lambda js: [j for j in js if only is None or j[0] in only]
        n = kept(jobs).index(job)
        pre, first, mid = len(kept(PRE)), len(kept(FIRST)), len(kept(MID))
        last = len(kept(MID)) - len(kept(group("qT", NX)))
        if stage_of == "pre":
            return n
        if stage_of == "first":
            return pre + n
        if stage_of == "tail":
            return pre + first + (NB - 2) * mid + last + n
        return b * mid + (pre + first - mid + n)

    JOBS = {"pre": PRE, "first": FIRST, "mid": MID, "tail": TAIL}

    def job_no(stage, b, name, n=0):
        return count(JOBS[stage], stage, b, (name, n))

    def act_no(stage, b, name, n=0):
        return count(JOBS[stage], stage, b, (name, n), BY_ACT)

    def slot_of(stage, name, n=0):
        for js in (PRE, FIRST, MID, TAIL):
            assert len(js) % 2 == 0
        return JOBS[stage].index((name, n)) % 2

    with ExitStack() as stack:
        def sb(name, shape, dt=F32):
            return stack.enter_context(nc.sbuf_tensor(name, shape, dt))

        def sem(name):
            return stack.enter_context(nc.semaphore(name))

        ident = sb("ident", [P, P])
        raw = sb("raw", [P, NT, D])
        CT = 3
        ctxT_h = sb("ctxT_h", [P, CT, LK], F32R)
        ctxT_l = sb("ctxT_l", [P, CT, LK], F32R)
        NR = 4
        val_h = sb("val_h", [P, NR, BANK], F32R)
        val_l = sb("val_l", [P, NR, BANK], F32R)
        nT_h = sb("nT_h", [P, KD, LQ], F32R)
        nT_l = sb("nT_l", [P, KD, LQ], F32R)
        xn = sb("xn", [QT, NQ, D])
        x2 = sb("x2", [QT, NQ, D])
        xT_st = sb("xT_st", [P, KD, LQ])
        ar_h = sb("ar_h", [P, KD, RE], F32R)
        ar_l = sb("ar_l", [P, KD, RE], F32R)
        gated = sb("gated", [QT, NQ, G])
        gT_st = sb("gT_st", [P, KG, LQ])
        prob = sb("prob", [QT, NQ, NT * P])
        eT_h = sb("eT_h", [P, NQ, NT, QT], F32R)
        eT_l = sb("eT_l", [P, NQ, NT, QT], F32R)
        hT = sb("hT", [RE, LQ])
        hn = sb("hn", [QT, NQ, RE])
        st1 = sb("st1", [QT, NQ, CH, STATS])
        st2 = sb("st2", [QT, NQ, CH, STATS])
        mv1 = sb("mv1", [QT, NQ, 2])
        mv2 = sb("mv2", [QT, NQ, 2])
        ve1 = sb("ve1", [QT, NQ])
        ve2 = sb("ve2", [QT, NQ])
        rs1 = sb("rs1", [QT, NQ])
        rs2 = sb("rs2", [QT, NQ])
        nb1 = sb("nb1", [QT, NQ])
        nb2 = sb("nb2", [QT, NQ])
        mhalf = sb("mhalf", [QT, NQ])
        nmax = sb("nmax", [QT, NQ])
        rsum = sb("rsum", [QT, NQ])
        rinv = sb("rinv", [QT, NQ])
        rank = sb("rank", [QT, E])
        t16 = [sb(f"t16_{i}", [QT, NQ, E]) for i in range(10)]
        t1 = [sb(f"t1_{i}", [QT, NQ]) for i in range(9)]

        scores = stack.enter_context(nc.psum_tensor("scores", [P, NQ, 2 * BANK], F32))
        work = stack.enter_context(nc.psum_tensor("work", [P, 2, 2 * BANK], F32))

        ident_ready = sem("ident_ready")
        consts_ready = sem("consts_ready")
        ar_loaded = sem("ar_loaded")
        raw_loaded = [sem(f"raw_loaded{c}") for c in range(CH)]
        xn_loaded = sem("xn_loaded")
        xres_loaded = sem("xres_loaded")
        filled = sem("filled")
        high_done = sem("high_done")
        drained = sem("drained")
        score_step = sem("score_step")
        max_ready = sem("max_ready")
        exp_done = sem("exp_done")
        rinv_ready = sem("rinv_ready")
        val_high = sem("val_high")
        val_ready = sem("val_ready")
        val_used = sem("val_used")
        pv_done = sem("pv_done")
        x2_done = sem("x2_done")
        x2_stored = sem("x2_stored")
        stat1, aggr1, var1, rstd1, bias1 = (sem(f"ln1_{n}") for n in ("stats", "aggr", "var", "rstd", "bias"))
        stat2, aggr2, var2, rstd2, bias2 = (sem(f"ln2_{n}") for n in ("stats", "aggr", "var", "rstd", "bias"))
        ln1_done = sem("ln1_done")
        ln2_done = sem("ln2_done")
        xT_staged = sem("xT_staged")
        xT_stored = sem("xT_stored")
        gT_stored = sem("gT_stored")
        route = sem("route")
        rexp_done = sem("rexp_done")
        gated_done = sem("gated_done")

        block = stack.enter_context(nc.Block())

        @block.sync
        def _(sp):
            def load_raw(b, c):
                cols = slice(c * BANK, (c + 1) * BANK)
                sp.dma_start(raw[:, 0:FULL, cols],
                             ctx[b, 0:FULL * P, cols].rearrange("(t p) d -> p t d", p=P)).then_inc(raw_loaded[c], 16)
                sp.dma_start(raw[0:REST, FULL, cols], ctx[b, FULL * P:LK, cols]).then_inc(raw_loaded[c], 16)

            def one(b, stage, last):
                if not last:
                    at_least(sp, filled, (job_no("pre", 0, "qT", NX - 1) if stage == "first"
                                          else first_or_mid_qT(b)) + 1)
                    sp.dma_start(xn[:, :, :], x_v[b + 1]).then_inc(xn_loaded, 16)
                if stage != "first":
                    sp.wait_ge(filled, job_no("mid", b, "x2T", NX - 1) + 1)
                sp.dma_start(x2[:, :, :], x_v[b]).then_inc(xres_loaded, 16)
                for c in range(CH):
                    if not last:
                        sp.wait_ge(val_ready, b * (CH * NT) + (c + 1) * NT)
                        load_raw(b + 1, c)
                    if stage != "first" and c == 0:
                        store_xT(b - 1)
                    if stage != "first" and c == 2:
                        store_gT(b - 1, drained_gT=job_no("mid", b, "gT", NG - 1) + 1)
                sp.wait_ge(x2_done, (b + 1) * (NQ * CH))
                sp.dma_start(x2_v[b], x2[:, :, :]).then_inc(x2_stored, 16)

            def first_or_mid_qT(b):
                return job_no("mid", b, "ctxT", 0) - 1

            def store_xT(b):
                sp.wait_ge(xT_staged, (b + 1) * NX)
                sp.dma_start(xT_d[:, :, bass.ds(b * LQ, LQ)], xT_st[:, :, :]).then_inc(xT_stored, 16)

            def store_gT(b, drained_gT):
                sp.wait_ge(drained, drained_gT)
                sp.dma_start(gT_d[:, :, bass.ds(b * LQ, LQ)], gT_st[:, :, :]).then_inc(gT_stored, 16)

            sp.dma_start(xn[:, :, :], x_v[0]).then_inc(xn_loaded, 16)
            an = gated[0:RE, :, :].rearrange("p q g -> p (q g)")
            sp.dma_start(an[0:R, :], A).then_inc(ar_loaded, 16)
            sp.dma_start(an[R:RE, :], router).then_inc(ar_loaded, 16)
            sp.wait_ge(consts_ready, 1)
            for c in range(CH):
                load_raw(0, c)
            one(0, "first", last=False)
            with sp.Fori(1, NB - 1) as b:
                one(b, "mid", last=False)
            one(NB - 1, "mid", last=True)
            sp.wait_ge(xT_staged, NB * NX)
            store_xT(NB - 1)
            store_gT(NB - 1, drained_gT=job_no("tail", NB, "gT", NG - 1) + 1)
            sp.wait_ge(x2_stored, NB * 16)
            sp.wait_ge(xT_stored, NB * 16)
            sp.wait_ge(gT_stored, NB * 16)

        @block.tensor
        def _(pe):
            def take(no):
                at_least(pe, drained, no - 1)

            def scores_of(b, stage):
                job = lambda k: job_no(stage, b, "ctxT", k)

                def transpose_block(k):
                    if k % (KD // CH) == 0:
                        pe.wait_ge(raw_loaded[k // (KD // CH)], b * 32 + 32)
                    take(job(k))
                    slot = slot_of(stage, "ctxT", k)
                    for t in range(NT):
                        rows = P if t < FULL else REST
                        last = pe.transpose(work[:, slot, t * P:t * P + rows],
                                            raw[0:rows, t, k * P:(k + 1) * P], ident[0:rows, 0:rows])
                    last.then_inc(filled, 1)

                transpose_block(0)
                transpose_block(1)
                if stage != "first":
                    pe.wait_ge(x2_done, b * (NQ * CH))
                for k in range(KD):
                    if k + 2 < KD:
                        transpose_block(k + 2)
                    pe.wait_ge(drained, job(k) + 1)
                    for q in range(NQ):
                        for h, (lo, hi) in enumerate(((0, BANK), (BANK, LK))):
                            out = scores[0:QT, q, lo:hi]
                            qh = nT_h[:, k, q * QT:(q + 1) * QT]
                            ql = nT_l[:, k, q * QT:(q + 1) * QT]
                            ch = ctxT_h[:, k % CT, lo:hi]
                            cl = ctxT_l[:, k % CT, lo:hi]
                            pe.matmul(out, qh, ch, start=(k == 0), stop=False)
                            pe.matmul(out, qh, cl, start=False, stop=False)
                            last = pe.matmul(out, ql, ch, start=False, stop=(k == KD - 1))
                    last.then_inc(score_step, 1)

            def transpose_rows(stage, b, name, src, blocks):
                for n in range(blocks // 4):
                    take(job_no(stage, b, name, n))
                    slot = slot_of(stage, name, n)
                    for i in range(4):
                        k = 4 * n + i
                        for q in range(NQ):
                            at = (i // 2) * BANK + (i % 2) * LQ + q * QT
                            last = pe.transpose(work[:, slot, at:at + QT],
                                                src[:, q, k * P:(k + 1) * P], ident[0:QT, 0:QT])
                    last.then_inc(filled, 1)

            def hidden_of(stage, b):
                take(job_no(stage, b, "hid"))
                out = work[0:RE, slot_of(stage, "hid"), 0:LQ]
                for k in range(KD):
                    if k % 4 == 0:
                        pe.wait_ge(drained, job_no(stage, b, "x2T", k // 4) + 1)
                    pe.matmul(out, ar_h[:, k, :], nT_h[:, k, :], start=(k == 0), stop=False)
                    pe.matmul(out, ar_h[:, k, :], nT_l[:, k, :], start=False, stop=False)
                    last = pe.matmul(out, ar_l[:, k, :], nT_h[:, k, :], start=False, stop=(k == KD - 1))
                last.then_inc(filled, 1)

            def x2T_of(stage, b, of):
                pe.wait_ge(ln2_done, (of + 1) * NQ)
                transpose_rows(stage, b, "x2T", x2, KD)

            def hidden_back(stage, b):
                take(job_no(stage, b, "hN"))
                pe.wait_ge(drained, job_no(stage, b, "hid") + 1)
                slot = slot_of(stage, "hN")
                for q in range(NQ):
                    last = pe.transpose(work[0:QT, slot, q * RE:(q + 1) * RE],
                                        hT[:, q * QT:(q + 1) * QT], ident[0:RE, 0:RE])
                last.then_inc(filled, 1)

            def exps_T(stage, b):
                for q in range(NQ):
                    pe.wait_ge(exp_done, b * NQ + q + 1)
                    take(job_no(stage, b, "eT", q))
                    slot = slot_of(stage, "eT", q)
                    for t in range(NT):
                        at = (t // 3) * BANK + (t % 3) * QT
                        last = pe.transpose(work[:, slot, at:at + QT],
                                            prob[:, q, t * P:(t + 1) * P], ident[0:QT, 0:QT])
                    last.then_inc(filled, 1)

            def outputs_of(stage, b):
                for c in range(CH):
                    if stage == "mid" and c == 2:
                        pe.wait_ge(gated_done, b * NQ)
                        transpose_rows(stage, b, "gT", gated, KG)
                    if c == 0:
                        pe.wait_ge(drained, job_no(stage, b, "eT", NQ - 1) + 1)
                    if c >= 2:
                        pe.wait_ge(x2_done, b * (NQ * CH) + NQ * (c - 1))
                    for t in range(NT):
                        e = c * NT + t
                        pe.wait_ge(val_ready, b * (CH * NT) + e + 1)
                        for q in range(NQ):
                            out = scores[0:QT, c % 2, q * BANK:(q + 1) * BANK]
                            eh, el = eT_h[:, q, t, :], eT_l[:, q, t, :]
                            vh, vl = val_h[:, e % NR, :], val_l[:, e % NR, :]
                            pe.matmul(out, eh, vh, start=(t == 0), stop=False)
                            pe.matmul(out, eh, vl, start=False, stop=False)
                            last = pe.matmul(out, el, vh, start=False, stop=(t == NT - 1))
                        last.then_inc(val_used, 1)

            def q_T(stage, b, of):
                pe.wait_ge(ln1_done, (of + 1) * NQ)
                transpose_rows(stage, b, "qT", xn, KD)

            def one(b, stage, last):
                scores_of(b, stage)
                if stage == "mid":
                    x2T_of(stage, b, of=b - 1)
                    hidden_of(stage, b)
                exps_T(stage, b)
                if stage == "mid":
                    hidden_back(stage, b)
                outputs_of(stage, b)
                if not last:
                    q_T(stage, b, of=b + 1)

            pe.wait_ge(ident_ready, 2)
            pe.wait_ge(ar_loaded, 32)
            an = gated[0:RE, :, :].rearrange("p q g -> p (q g)")
            for n in range(2):
                for i in range(8):
                    k = 8 * n + i
                    at = (i // 4) * BANK + (i % 4) * RE
                    last = pe.transpose(work[:, n, at:at + RE], an[:, k * P:(k + 1) * P], ident[0:RE, 0:RE])
                last.then_inc(filled, 1)
            q_T("pre", 0, of=0)
            one(0, "first", last=False)
            with pe.Fori(1, NB - 1) as b:
                one(b, "mid", last=False)
            one(NB - 1, "mid", last=True)
            x2T_of("tail", NB, of=NB - 1)
            hidden_of("tail", NB)
            hidden_back("tail", NB)
            pe.wait_ge(gated_done, NB * NQ)
            transpose_rows("tail", NB, "gT", gated, KG)

        @block.scalar
        def _(act):
            def high(stage, b, name, n, out, cols, width):
                act.wait_ge(filled, job_no(stage, b, name, n) + 1)
                src = work[:, slot_of(stage, name, n), :].rearrange("p (k c) -> p k c", k=cols)[:, :, 0:width]
                act.activation(out, src, ACT.Copy).then_inc(high_done, 1)

            def ctx_high(stage, b, k):
                if k >= CT:
                    act.wait_ge(score_step, b * KD + k - CT + 1)
                act.wait_ge(filled, job_no(stage, b, "ctxT", k) + 1)
                act.activation(ctxT_h[:, k % CT, :], work[:, slot_of(stage, "ctxT", k), 0:LK],
                               ACT.Copy).then_inc(high_done, 1)

            def four_blocks(tile, n):
                return tile[:, 4 * n:4 * n + 4, :].rearrange("p (k i) c -> p k (i c)", k=2)

            def normalise(tile, q, rstd, bias, sem_done):
                act.activation(tile[:, q, :], tile[:, q, :], ACT.Identity, bias=bias[:, q:q + 1],
                               scale=rstd[:, q:q + 1]).then_inc(sem_done, 1)

            def value_high(b, e):
                at_least(act, val_used, b * (CH * NT) + e - NR + 1)
                c, t = e // NT, e % NT
                act.activation(val_h[:, e % NR, :], raw[:, t, c * BANK:(c + 1) * BANK],
                               ACT.Copy).then_inc(val_high, 1)

            def exponentials(b):
                for q in range(NQ):
                    act.wait_ge(max_ready, b * NQ + q + 1)
                    act.activation(prob[:, q, 0:LK], scores[0:QT, q, 0:LK], ACT.Exp, bias=nmax[:, q:q + 1],
                                   scale=1.0, accum_out=rsum[:, q:q + 1]).then_inc(exp_done, 1)

            def routing_exp(of):
                act.wait_ge(route, of * ROUTE + 2)
                act.activation(t16[1][:, :, :], t16[0][:, :, :], ACT.Exp).then_inc(rexp_done, 1)

            def one(b, stage, last):
                for k in range(KD):
                    ctx_high(stage, b, k)
                    if stage == "mid" and k in (10, 11):
                        if k == 10:
                            act.wait_ge(bias2, b)
                            act.wait_ge(x2_stored, b * 16)
                        normalise(x2, k - 10, rs2, nb2, ln2_done)
                if stage == "mid":
                    for n in range(NX):
                        high(stage, b, "x2T", n, four_blocks(nT_h, n), 2, 2 * LQ)
                exponentials(b)
                for e in range(NR):
                    value_high(b, e)
                for q in range(NQ):
                    high(stage, b, "eT", q, eT_h[:, q, :, :].rearrange("p (k i) c -> p k (i c)", k=2), 2, 3 * QT)
                for e in range(NR, CH * NT):
                    value_high(b, e)
                    if stage == "mid" and e == NR + 3:
                        routing_exp(b - 1)
                    if not last and e in (18, 20):
                        if e == 18:
                            act.wait_ge(bias1, b + 2)
                        normalise(xn, (e - 18) // 2, rs1, nb1, ln1_done)
                if not last:
                    if stage == "mid":
                        act.wait_ge(xT_staged, b * NX)
                    for n in range(NX):
                        high(stage, b, "qT", n, four_blocks(nT_h, n), 2, 2 * LQ)

            for n in range(2):
                high("pre", 0, "arT", n, ar_h[:, 8 * n:8 * n + 8, :].rearrange("p (k i) c -> p k (i c)", k=2), 2, 4 * RE)
            act.wait_ge(bias1, 1)
            for q in range(NQ):
                normalise(xn, q, rs1, nb1, ln1_done)
            for n in range(NX):
                high("pre", 0, "qT", n, four_blocks(nT_h, n), 2, 2 * LQ)
            one(0, "first", last=False)
            with act.Fori(1, NB - 1) as b:
                one(b, "mid", last=False)
            one(NB - 1, "mid", last=True)
            act.wait_ge(bias2, NB)
            act.wait_ge(x2_stored, NB * 16)
            for q in range(NQ):
                normalise(x2, q, rs2, nb2, ln2_done)
            for n in range(NX):
                high("tail", NB, "x2T", n, four_blocks(nT_h, n), 2, 2 * LQ)
            routing_exp(NB - 1)

        @block.vector
        def _(dve):
            def low(stage, b, name, n, high_part, low_part, cols, width):
                dve.wait_ge(high_done, act_no(stage, b, name, n) + 1)
                src = work[:, slot_of(stage, name, n), :].rearrange("p (k c) -> p k c", k=cols)[:, :, 0:width]
                dve.tensor_tensor(low_part, src, as_f32(high_part), ALU.subtract).then_inc(drained, 1)

            def ctx_low(stage, b, k):
                dve.wait_ge(high_done, act_no(stage, b, "ctxT", k) + 1)
                dve.tensor_tensor(ctxT_l[:, k % CT, :], work[:, slot_of(stage, "ctxT", k), 0:LK],
                                  as_f32(ctxT_h[:, k % CT, :]), ALU.subtract).then_inc(drained, 1)

            def four_blocks(tile, n):
                return tile[:, 4 * n:4 * n + 4, :].rearrange("p (k i) c -> p k (i c)", k=2)

            def value_low(b, e):
                c, t = e // NT, e % NT
                dve.wait_ge(val_high, b * (CH * NT) + e + 1)
                dve.tensor_tensor(val_l[:, e % NR, :], raw[:, t, c * BANK:(c + 1) * BANK],
                                  as_f32(val_h[:, e % NR, :]), ALU.subtract).then_inc(val_ready, 1)

            def stats(tile, st, sem_stat, i):
                q, c = i // CH, i % CH
                dve.bn_stats(st[:, q, c, :], tile[:, q, c * BANK:(c + 1) * BANK]).then_inc(sem_stat, 1)

            def aggregate(st, mv, sem_aggr):
                for q in range(NQ):
                    dve.bn_aggr(mv[:, q, :], st[:, q, :, :].rearrange("p c s -> p (c s)")).then_inc(sem_aggr, 1)

            def variance(mv, ve, sem_aggr, sem_var, n):
                dve.wait_ge(sem_aggr, n * NQ + NQ)
                dve.tensor_scalar(ve[:, :], mv[:, :, 1], EPS, None, ALU.add).then_inc(sem_var, 1)

            def shift(mv, rs, nb, sem_rstd, sem_bias, n):
                dve.wait_ge(sem_rstd, n + 1)
                dve.scalar_tensor_tensor(nb[:, :], mv[:, :, 0], -1.0, rs[:, :], ALU.mult,
                                         ALU.mult).then_inc(sem_bias, 1)

            def row_max(b):
                for q in range(NQ):
                    if q == 0:
                        dve.wait_ge(score_step, b * KD + KD)
                    dve.reduce_max(nmax[:, q:q + 1], scores[0:QT, q, 0:LK], AX.X,
                                   negate=True).then_inc(max_ready, 1)

            def residual(b, c):
                if c == 0:
                    dve.wait_ge(exp_done, b * NQ + NQ)
                    dve.reciprocal(rinv[:, :], rsum[:, :]).then_inc(rinv_ready, 1)
                    dve.wait_ge(xres_loaded, b * 16 + 16)
                    dve.wait_ge(rinv_ready, b + 1)
                dve.wait_ge(val_used, b * (CH * NT) + (c + 1) * NT)
                for q in range(NQ):
                    cols = slice(c * BANK, (c + 1) * BANK)
                    dve.scalar_tensor_tensor(x2[:, q, cols], scores[0:QT, c % 2, q * BANK:(q + 1) * BANK],
                                             rinv[:, q:q + 1], x2[:, q, cols], ALU.mult,
                                             ALU.add).then_inc(x2_done, 1)

            def hidden_out(stage, b):
                dve.wait_ge(filled, job_no(stage, b, "hid") + 1)
                dve.tensor_copy(hT[:, :], work[0:RE, slot_of(stage, "hid"), 0:LQ]).then_inc(drained, 1)

            def hidden_back(stage, b):
                dve.wait_ge(filled, job_no(stage, b, "hN") + 1)
                dve.tensor_copy(hn[:, :, :].rearrange("p q r -> p (q r)"),
                                work[0:QT, slot_of(stage, "hN"), 0:NQ * RE]).then_inc(drained, 1)

            def wide(v):
                return v.unsqueeze(2).to_broadcast([QT, NQ, E])

            rank_w = rank[:, :].unsqueeze(1).to_broadcast([QT, NQ, E])

            def route_steps(stage, b, of):
                logits = hn[:, :, R:RE]
                z, ez, p, eq1, key1, one1, p_rest, eq2, key2, one2 = (t[:, :, :] for t in t16)
                lmax, s, rs, m1, k1, m2, k2, den, rden = (t[:, :] for t in t1)
                v = dve
                return [
                    lambda: v.reduce_max(lmax, logits, AX.X),
                    lambda: v.tensor_tensor(z, logits, wide(lmax), ALU.subtract),
                    lambda: v.reduce_sum(s, ez, AX.X),
                    lambda: v.reciprocal(rs, s),
                    lambda: v.tensor_tensor(p, ez, wide(rs), ALU.mult),
                    lambda: v.reduce_max(m1, p, AX.X),
                    lambda: v.tensor_tensor(eq1, p, wide(m1), ALU.is_equal),
                    lambda: v.tensor_tensor(key1, eq1, rank_w, ALU.mult),
                    lambda: v.reduce_max(k1, key1, AX.X),
                    lambda: v.tensor_tensor(one1, key1, wide(k1), ALU.is_equal),
                    lambda: v.scalar_tensor_tensor(p_rest, one1, -2.0, p, ALU.mult, ALU.add),
                    lambda: v.reduce_max(m2, p_rest, AX.X),
                    lambda: v.tensor_tensor(eq2, p_rest, wide(m2), ALU.is_equal),
                    lambda: v.tensor_tensor(key2, eq2, rank_w, ALU.mult),
                    lambda: v.reduce_max(k2, key2, AX.X),
                    lambda: v.tensor_tensor(one2, key2, wide(k2), ALU.is_equal),
                    lambda: v.tensor_tensor(one1, one1, one2, ALU.add),
                    lambda: v.tensor_tensor(den, m1, m2, ALU.add),
                    lambda: v.tensor_scalar(den, den, TOP_EPS, 1.0 / SCALING, ALU.add, ALU.mult),
                    lambda: v.reciprocal(rden, den),
                    lambda: v.tensor_tensor(z, one1, p, ALU.mult),
                    lambda: v.tensor_tensor(ez, z, wide(rden), ALU.mult),
                ]

            def run_route(stage, b, of, lo, hi):
                steps = route_steps(stage, b, of)
                assert len(steps) == ROUTE
                for n in range(lo, hi):
                    if n == 0:
                        dve.wait_ge(drained, job_no(stage, b, "hN") + 1)
                    else:
                        dve.wait_ge(route, of * ROUTE + n)
                    if n == 2:
                        dve.wait_ge(rexp_done, of + 1)
                    steps[n]().then_inc(route, 1)

            def gated_T(stage, b, of):
                if not (isinstance(of, int) and of == 0):
                    if stage == "mid":
                        at_least(dve, gT_stored, of * 16)
                    else:
                        dve.wait_ge(gT_stored, of * 16)
                for n in range(NG):
                    dve.wait_ge(filled, job_no(stage, b, "gT", n) + 1)
                    src = work[:, slot_of(stage, "gT", n), :].rearrange("p (k c) -> p k c", k=2)[:, :, 0:2 * LQ]
                    dve.tensor_copy(four_blocks(gT_st, n), src).then_inc(drained, 1)

            def one(b, stage, last):
                mid = stage == "mid"
                for k in range(KD):
                    ctx_low(stage, b, k)
                    if mid:
                        if k < 8:
                            if k == 0:
                                dve.wait_ge(x2_done, b * (NQ * CH))
                            stats(x2, st2, stat2, k)
                            if k == 7:
                                dve.wait_ge(stat2, b * (NQ * CH))
                        elif k == 8:
                            aggregate(st2, mv2, aggr2)
                            variance(mv2, ve2, aggr2, var2, b - 1)
                        elif k == 9:
                            shift(mv2, rs2, nb2, rstd2, bias2, b - 1)
                if mid:
                    for n in range(NX):
                        low(stage, b, "x2T", n, four_blocks(nT_h, n), four_blocks(nT_l, n), 2, 2 * LQ)
                row_max(b)
                for e in range(NR):
                    value_low(b, e)
                if mid:
                    hidden_out(stage, b)
                for q in range(NQ):
                    three = lambda tile: tile[:, q, :, :].rearrange("p (k i) c -> p k (i c)", k=2)
                    low(stage, b, "eT", q, three(eT_h), three(eT_l), 2, 3 * QT)
                if mid:
                    hidden_back(stage, b)
                for e in range(NR, CH * NT):
                    value_low(b, e)
                    c, t = e // NT, e % NT
                    if mid and 4 <= e < 4 + len(ROUTE_CUTS) - 1:
                        run_route(stage, b, b - 1, ROUTE_CUTS[e - 4], ROUTE_CUTS[e - 3])
                    if c >= 1 and t == 2:
                        residual(b, c - 1)
                    if mid and e == 16:
                        gated_T(stage, b, b - 1)
                    if not last:
                        if 9 <= e < 17:
                            if e == 9:
                                dve.wait_ge(xn_loaded, b * 16 + 32)
                            stats(xn, st1, stat1, e - 9)
                            if e == 16:
                                dve.wait_ge(stat1, (b + 2) * (NQ * CH))
                        elif e == 17:
                            aggregate(st1, mv1, aggr1)
                            variance(mv1, ve1, aggr1, var1, b + 1)
                            shift(mv1, rs1, nb1, rstd1, bias1, b + 1)
                residual(b, CH - 1)
                if not last:
                    for n in range(NX):
                        low(stage, b, "qT", n, four_blocks(nT_h, n), four_blocks(nT_l, n), 2, 2 * LQ)

            dve.memset(raw[96:P, FULL, :], 0.0).then_inc(consts_ready, 1)
            dve.memset(prob[:, :, LK:NT * P], 0.0).then_inc(consts_ready, 1)
            for e in range(E):
                dve.memset(rank[:, e:e + 1], float(E - e)).then_inc(consts_ready, 1)
            dve.wait_ge(xn_loaded, 16)
            for i in range(NQ * CH):
                stats(xn, st1, stat1, i)
            dve.wait_ge(stat1, NQ * CH)
            aggregate(st1, mv1, aggr1)
            variance(mv1, ve1, aggr1, var1, 0)
            shift(mv1, rs1, nb1, rstd1, bias1, 0)
            for n in range(2):
                eight = lambda tile: tile[:, 8 * n:8 * n + 8, :].rearrange("p (k i) c -> p k (i c)", k=2)
                low("pre", 0, "arT", n, eight(ar_h), eight(ar_l), 2, 4 * RE)
            for n in range(NX):
                low("pre", 0, "qT", n, four_blocks(nT_h, n), four_blocks(nT_l, n), 2, 2 * LQ)
            dve.wait_ge(consts_ready, 2 + E)
            one(0, "first", last=False)
            with dve.Fori(1, NB - 1) as b:
                one(b, "mid", last=False)
            one(NB - 1, "mid", last=True)
            dve.wait_ge(x2_done, NB * NQ * CH)
            for i in range(NQ * CH):
                stats(x2, st2, stat2, i)
            dve.wait_ge(stat2, NB * NQ * CH)
            aggregate(st2, mv2, aggr2)
            variance(mv2, ve2, aggr2, var2, NB - 1)
            shift(mv2, rs2, nb2, rstd2, bias2, NB - 1)
            for n in range(NX):
                low("tail", NB, "x2T", n, four_blocks(nT_h, n), four_blocks(nT_l, n), 2, 2 * LQ)
            hidden_out("tail", NB)
            hidden_back("tail", NB)
            run_route("tail", NB, NB - 1, 0, ROUTE)
            gated_T("tail", NB, NB - 1)

        @block.gpsimd
        def _(pool):
            def reciprocal_root(ve, rs, sem_var, sem_rstd, n):
                pool.wait_ge(sem_var, n + 1)
                pool.tensor_tensor(rs[:, :], ve[:, :], mhalf[:, :], ALU.pow).then_inc(sem_rstd, 1)

            def stage_xT(stage, b, of):
                if not (isinstance(of, int) and of == 0):
                    at_least(pool, xT_stored, of * 16)
                for n in range(NX):
                    pool.wait_ge(drained, job_no(stage, b, "x2T", n) + 1)
                    cut = slice(4 * n, 4 * n + 4)
                    pool.tensor_tensor(xT_st[:, cut, :], as_f32(nT_h[:, cut, :]), as_f32(nT_l[:, cut, :]),
                                       ALU.add).then_inc(xT_staged, 1)

            def gate(of):
                pool.wait_ge(route, of * ROUTE + ROUTE)
                for q in range(NQ):
                    pool.tensor_tensor(gated[:, q, :].rearrange("p (e r) -> p e r", e=E),
                                       t16[1][:, q, :].unsqueeze(2).to_broadcast([QT, E, R]),
                                       hn[:, q, 0:R].unsqueeze(1).to_broadcast([QT, E, R]),
                                       ALU.mult).then_inc(gated_done, 1)

            build_identity(pool, ident, ident_ready)
            pool.memset(mhalf[:, :], -0.5).then_inc(ident_ready, 1)
            pool.wait_ge(ident_ready, 3)
            reciprocal_root(ve1, rs1, var1, rstd1, 0)
            reciprocal_root(ve1, rs1, var1, rstd1, 1)
            with pool.Fori(1, NB - 1) as b:
                reciprocal_root(ve2, rs2, var2, rstd2, b - 1)
                stage_xT("mid", b, b - 1)
                gate(b - 1)
                reciprocal_root(ve1, rs1, var1, rstd1, b + 1)
            reciprocal_root(ve2, rs2, var2, rstd2, NB - 2)
            stage_xT("mid", NB - 1, NB - 2)
            gate(NB - 2)
            reciprocal_root(ve2, rs2, var2, rstd2, NB - 1)
            stage_xT("tail", NB, NB - 1)
            gate(NB - 1)


ROUTE = 22
ROUTE_CUTS = (0, 2, 5, 8, 11, 14, 17, 20, ROUTE)


def linear_phase(nc, W, bias, Bw, x2_d, xT_d, gT_d, out):
    D = W.shape[0]
    E, _, R = Bw.shape
    T = out.shape[0]
    NT = T // P
    KW = W.shape[1] // P
    KG = E * R // P
    K = KW + KG
    NC = D // BANK
    OT = BANK // P
    PK = 4
    NP = K // PK
    WP = KW // PK
    RING = 3
    EP = PK * P // R
    PSR = 4
    assert T % P == 0 and NT % 2 == 0 and NP % RING == 0 and K % PSR == 0

    with ExitStack() as stack:
        def sb(name, shape, dt=F32):
            return stack.enter_context(nc.sbuf_tensor(name, shape, dt))

        def sem(name):
            return stack.enter_context(nc.semaphore(name))

        ident = sb("ident2", [P, P])
        w_h = sb("w_h", [P, K, BANK], F32R)
        w_l = sb("w_l", [P, K, BANK], F32R)
        piece = sb("piece", [P, RING, OT, PK * P])
        a_raw = sb("a_raw", [P, K, P])
        a_h = sb("a_h", [P, 2, K, P], F32R)
        a_l = sb("a_l", [P, 2, K, P], F32R)
        res = sb("res", [P, 2, BANK])
        bias_b = sb("bias_b", [P, BANK])

        acc = stack.enter_context(nc.psum_tensor("acc", [P, 2, BANK], F32))
        wT = stack.enter_context(nc.psum_tensor("wT", [P, PSR, BANK], F32))

        ident_ready = sem("ident2_ready")
        piece_loaded = [sem(f"piece_loaded{s}") for s in range(RING)]
        w_filled = sem("w_filled")
        w_high = sem("w_high")
        w_ready = sem("w_ready")
        ax_loaded = sem("ax_loaded")
        ag_loaded = sem("ag_loaded")
        ax_high = sem("ax_high")
        ag_high = sem("ag_high")
        ax_low = sem("ax_low")
        ag_low = sem("ag_low")
        res_loaded = [sem(f"res_loaded{i}") for i in range(2)]
        bias_loaded = sem("bias_loaded")
        res_ready = sem("res_ready")
        tile_done = sem("tile_done")
        out_ready = sem("out_ready")
        out_stored = [sem(f"out_stored{i}") for i in range(2)]

        LOADS = [1 if p < WP else OT for p in range(NP)]

        def piece_count(c, p):
            mine = [j for j in range(NP) if j % RING == p % RING]
            total = 16 * sum(LOADS[j] for j in mine)
            return c * total + 16 * sum(LOADS[j] for j in mine if j <= p)

        def load_piece(eng, c, p):
            s = p % RING
            if p < WP:
                src = W[bass.ds(c * BANK, BANK), p * PK * P:(p + 1) * PK * P].rearrange("(o p) i -> p o i", p=P)
                eng.dma_start(piece[:, s, :, :], src).then_inc(piece_loaded[s], 16)
            else:
                for o in range(OT):
                    e0 = (p - WP) * EP
                    src = Bw[e0:e0 + EP, bass.ds(c * BANK + o * P, P), :].rearrange("e p r -> p e r")
                    dst = piece[:, s, o, :].rearrange("p (e r) -> p e r", e=EP)
                    eng.dma_start(dst, src).then_inc(piece_loaded[s], 16)

        block = stack.enter_context(nc.Block())

        @block.sync
        def _(sp):
            def load_tile(c, t, par):
                g = c * NT + t
                at_least(sp, ax_low, g)
                sp.dma_start(a_raw[:, 0:KW, :], xT_d[:, :, bass.ds(t * P, P)]).then_inc(ax_loaded, 16)
                at_least(sp, ag_low, g)
                sp.dma_start(a_raw[:, KW:K, :], gT_d[:, :, bass.ds(t * P, P)]).then_inc(ag_loaded, 16)

            def load_res(c, t, par, half):
                at_least(sp, out_stored[par], half * 16)
                sp.dma_start(res[:, par, :], x2_d[bass.ds(t * P, P), bass.ds(c * BANK, BANK)]).then_inc(
                    res_loaded[par], 16)

            def load_bias(c):
                at_least(sp, res_ready, c * NT)
                sp.dma_start(bias_b[:, :], bias[bass.ds(c * BANK, BANK)].unsqueeze(0).to_broadcast([P, BANK])
                             ).then_inc(bias_loaded, 16)

            def pair(c, i):
                for par in range(2):
                    load_tile(c, i * 2 + par, par)
                    load_res(c, i * 2 + par, par, c * (NT // 2) + i)

            def chunk(c):
                load_bias(c)
                if isinstance(c, int) and c == 0:
                    pair(c, 0)
                    with sp.Fori(1, NT // 2) as i:
                        pair(c, i)
                else:
                    with sp.Fori(0, NT // 2) as i:
                        pair(c, i)

            chunk(0)
            with sp.Fori(1, NC) as c:
                chunk(c)

        @block.tensor
        def _(pe):
            def transpose_weights(c, k):
                p, kk = k // PK, k % PK
                if kk == 0:
                    pe.wait_ge(piece_loaded[p % RING], piece_count(c, p))
                if not (isinstance(c, int) and c == 0 and k < PSR):
                    pe.wait_ge(w_ready, c * K + k - PSR + 1)
                for o in range(OT):
                    last = pe.transpose(wT[:, k % PSR, o * P:(o + 1) * P],
                                        piece[:, p % RING, o, kk * P:(kk + 1) * P], ident[:, :])
                last.then_inc(w_filled, 1)

            def block_products(c, k, par):
                out = acc[:, par, :]
                pe.matmul(out, a_h[:, par, k, :], w_h[:, k, :], start=(k == 0), stop=False)
                pe.matmul(out, a_h[:, par, k, :], w_l[:, k, :], start=False, stop=False)
                return pe.matmul(out, a_l[:, par, k, :], w_h[:, k, :], start=False, stop=(k == K - 1))

            def start_tile(g):
                if not isinstance(g, int) or g >= 2:
                    at_least(pe, out_ready, g - 1)
                pe.wait_ge(ax_low, g + 1)

            def tile(c, g, par, first=False):
                start_tile(g)
                for k in range(K):
                    if k == KW:
                        pe.wait_ge(ag_low, g + 1)
                    if first:
                        pe.wait_ge(w_ready, c * K + k + 1)
                    last = block_products(c, k, par)
                last.then_inc(tile_done, 1)

            def chunk(c, more):
                g0 = c * NT
                tile(c, g0, 0, first=True)
                tile(c, g0 + 1, 1)
                with pe.Fori(1, NT // 2 - 1) as i:
                    tile(c, g0 + i * 2, 0)
                    tile(c, g0 + i * 2 + 1, 1)
                tile(c, g0 + NT - 2, 0)
                if not more:
                    tile(c, g0 + NT - 1, 1)
                    return
                start_tile(g0 + NT - 1)
                for k in range(K):
                    if k == KW:
                        pe.wait_ge(ag_low, g0 + NT)
                    last = block_products(c, k, 1)
                    if k == K - 1:
                        last.then_inc(tile_done, 1)
                    transpose_weights(c + 1, k)

            pe.wait_ge(ident_ready, 2)
            for k in range(K):
                transpose_weights(0, k)
            chunk(0, True)
            with pe.Fori(1, NC - 1) as c:
                chunk(c, True)
            chunk(NC - 1, False)

        @block.scalar
        def _(act):
            def weight_high(c, k, next_too):
                act.wait_ge(w_filled, c * K + k + 1)
                act.activation(w_h[:, k, :], wT[:, k % PSR, :], ACT.Copy).then_inc(w_high, 1)
                if k % PK == PK - 1:
                    p = k // PK
                    if p + RING < NP:
                        load_piece(act, c, p + RING)
                    elif next_too:
                        load_piece(act, c + 1, p + RING - NP)

            def split_high(g, par):
                if not isinstance(g, int) or g >= 2:
                    at_least(act, tile_done, g - 1)
                act.wait_ge(ax_loaded, g * 16 + 16)
                act.activation(a_h[:, par, 0:KW, :], a_raw[:, 0:KW, :], ACT.Copy).then_inc(ax_high, 1)
                act.wait_ge(ag_loaded, g * 16 + 16)
                act.activation(a_h[:, par, KW:K, :], a_raw[:, KW:K, :], ACT.Copy).then_inc(ag_high, 1)

            def store(c, t, par):
                act.wait_ge(out_ready, c * NT + t + 1)
                act.dma_start(out[bass.ds(t * P, P), bass.ds(c * BANK, BANK)], res[:, par, :]).then_inc(
                    out_stored[par], 16)

            def chunk(c, first, more):
                g0 = c * NT
                if first:
                    split_high(g0 + 1, 1)
                    store(c, 0, 0)
                    split_high(g0 + 2, 0)
                    store(c, 1, 1)
                    lo = 1
                else:
                    lo = 0
                with act.Fori(lo, NT // 2 - 1) as i:
                    split_high(g0 + i * 2 + 1, 1)
                    store(c, i * 2, 0)
                    split_high(g0 + i * 2 + 2, 0)
                    store(c, i * 2 + 1, 1)
                split_high(g0 + NT - 1, 1)
                store(c, NT - 2, 0)
                if more:
                    split_high(g0 + NT, 0)
                    for k in range(K):
                        weight_high(c + 1, k, next_too=not (isinstance(c, int) and c == NC - 2))
                store(c, NT - 1, 1)

            for p in range(RING):
                load_piece(act, 0, p)
            split_high(0, 0)
            for k in range(K):
                weight_high(0, k, True)
            chunk(0, True, True)
            with act.Fori(1, NC - 2) as c:
                chunk(c, False, True)
            chunk(NC - 2, False, True)
            chunk(NC - 1, False, False)
            for par in range(2):
                act.wait_ge(out_stored[par], NC * (NT // 2) * 16)

        @block.vector
        def _(dve):
            def weight_low(c, k):
                dve.wait_ge(w_high, c * K + k + 1)
                dve.tensor_tensor(w_l[:, k, :], wT[:, k % PSR, :], as_f32(w_h[:, k, :]),
                                  ALU.subtract).then_inc(w_ready, 1)

            def split_low(g, par):
                dve.wait_ge(ax_high, g + 1)
                dve.tensor_tensor(a_l[:, par, 0:KW, :], a_raw[:, 0:KW, :], as_f32(a_h[:, par, 0:KW, :]),
                                  ALU.subtract).then_inc(ax_low, 1)

            def finish(g, par):
                dve.wait_ge(res_ready, g + 1)
                dve.wait_ge(tile_done, g + 1)
                dve.tensor_tensor(res[:, par, :], acc[:, par, :], res[:, par, :], ALU.add).then_inc(out_ready, 1)

            def chunk(c, more):
                g0 = c * NT
                with dve.Fori(0, NT // 2 - 1) as i:
                    split_low(g0 + i * 2 + 1, 1)
                    finish(g0 + i * 2, 0)
                    split_low(g0 + i * 2 + 2, 0)
                    finish(g0 + i * 2 + 1, 1)
                split_low(g0 + NT - 1, 1)
                finish(g0 + NT - 2, 0)
                if more:
                    split_low(g0 + NT, 0)
                    for k in range(K):
                        weight_low(c + 1, k)
                finish(g0 + NT - 1, 1)

            split_low(0, 0)
            for k in range(K):
                weight_low(0, k)
            with dve.Fori(0, NC - 1) as c:
                chunk(c, True)
            chunk(NC - 1, False)

        @block.gpsimd
        def _(pool):
            def tile(c, g, par, half):
                pool.wait_ge(ag_high, g + 1)
                pool.tensor_tensor(a_l[:, par, KW:K, :], a_raw[:, KW:K, :], as_f32(a_h[:, par, KW:K, :]),
                                   ALU.subtract).then_inc(ag_low, 1)
                pool.wait_ge(bias_loaded, c * 16 + 16)
                pool.wait_ge(res_loaded[par], half * 16 + 16)
                pool.tensor_tensor(res[:, par, :], res[:, par, :], bias_b[:, :], ALU.add).then_inc(res_ready, 1)

            build_identity(pool, ident, ident_ready)
            with pool.Fori(0, NC) as c:
                with pool.Fori(0, NT // 2) as i:
                    for par in range(2):
                        tile(c, c * NT + i * 2 + par, par, c * (NT // 2) + i)


def xattn_ffn_kernel(nc, x, ctx_4096, L0_ffn_base_w, L0_ffn_base_b, L0_ffn_A, L0_ffn_B, L0_ffn_router_w, out):
    NB, LQ, D = x.shape
    T = NB * LQ
    E, _, R = L0_ffn_B.shape
    x2_d = nc.dram_tensor("x2_scratch", [T, D], F32).ap()
    xT_d = nc.dram_tensor("xT_scratch", [P, D // P, T], F32).ap()
    gT_d = nc.dram_tensor("gT_scratch", [P, E * R // P, T], F32).ap()
    attention_phase(nc, x, ctx_4096, L0_ffn_A, L0_ffn_router_w, x2_d, xT_d, gT_d)
    linear_phase(nc, L0_ffn_base_w, L0_ffn_base_b, L0_ffn_B, x2_d, xT_d, gT_d,
                 out.rearrange("b s d -> (b s) d"))


_INS = ["x", "ctx_4096", "L0_ffn_base_w", "L0_ffn_base_b", "L0_ffn_A", "L0_ffn_B", "L0_ffn_router_w"]
_OUTS = [((8, 224, 2048), "float32")]


def kernel(**inputs):
    import numpy as _np
    import concourse.bacc as _bacc
    from concourse import mybir as _mybir
    from concourse.bass_utils import run_bass_kernel_spmd as _run

    nc = _bacc.Bacc("TRN2", target_bir_lowering=False, num_devices=1)
    arrays, args = {}, []
    for name in _INS:
        a = _np.ascontiguousarray(inputs[name])
        arrays[f"in_{name}_dram"] = a
        args.append(nc.dram_tensor(f"in_{name}_dram", a.shape, _mybir.dt.from_np(a.dtype), kind="ExternalInput").ap())
    for i, (shape, dtype) in enumerate(_OUTS):
        dt = _mybir.dt.from_np(_np.dtype(dtype))
        args.append(nc.dram_tensor(f"out_{i}_dram", shape, dt, kind="ExternalOutput").ap())
    xattn_ffn_kernel(nc, *args)
    r = _run(nc, [arrays], core_ids=[0])
    got = tuple(r.results[0][f"out_{i}_dram"] for i in range(len(_OUTS)))
    return got[0]
```

```python
from contextlib import ExitStack

import concourse.bass as bass
from concourse import mybir

ALU = mybir.AluOpType
ACT = mybir.ActivationFunctionType
AX = mybir.AxisListType
F32 = mybir.dt.float32
F32R = mybir.dt.float32r

P = 128
BANK = 512
EPS = 1e-5
TOP_EPS = 1e-6
SCALING = 0.5
STATS = 6


def as_f32(ap):
    return ap.bitcast(F32)


def at_least(eng, sem, value):
    if isinstance(value, int) and value <= 0:
        return
    eng.wait_ge(sem, value)


def build_identity(pool, ident, sem):
    pool.memset(ident[:, :], 0.0).then_inc(sem, 1)
    pool.wait_ge(sem, 1)
    pool.affine_select(out=ident[:, :], in_=ident[:, :], compare_op=ALU.not_equal, fill=1.0, base=0,
                       pattern=[[-1, P]], channel_multiplier=1).then_inc(sem, 1)


def attention_phase(nc, x, ctx, A, router, x2_d, xT_d, gT_d):
    NB, LQ, D = x.shape
    LK = ctx.shape[1]
    R, E = A.shape[0], router.shape[0]
    QT = LQ // 2
    NQ = 2
    KD = D // P
    NT = -(-LK // P)
    FULL = LK // P
    REST = LK - FULL * P
    CH = D // BANK
    RE = R + E
    G = R * E
    KG = G // P
    LOGITS = 16
    assert LQ == NQ * QT and D == CH * BANK and RE <= P and G % P == 0

    x_v = x.rearrange("b (q p) d -> b p q d", p=QT)
    x2_v = x2_d.rearrange("(b q p) d -> b p q d", q=NQ, p=QT)

    NX = KD // 4
    NG = KG // 4
    def group(name, n):
        return [(name, i) for i in range(n)]
    BEFORE = group("ctxT", KD)
    OLD = [("hid", 0), ("hN", 0)]
    JOBS = {
        "pre": group("arT", 2) + group("qT", NX),
        "first": BEFORE + group("eT", NQ) + group("qT", NX),
        "mid": BEFORE + group("x2T", NX) + group("eT", NQ) + OLD + group("qT", NX) + group("gT", NG),
        "last": BEFORE + group("x2T", NX) + group("eT", NQ) + OLD + group("gT", NG),
        "tail": group("x2T", NX) + OLD + group("gT", NG),
    }
    BY_ACT = ("arT", "qT", "ctxT", "x2T", "eT")
    TIMES = {"pre": 1, "first": 1, "mid": NB - 2, "last": 1, "tail": 1}
    assert all(len(jobs) % 2 == 0 for jobs in JOBS.values())

    def number(stage, b, job, kinds):
        of = {name: [j for j in jobs if j[0] in kinds] for name, jobs in JOBS.items()}
        before = 0
        for name in JOBS:
            if name == stage:
                break
            before += TIMES[name] * len(of[name])
        n = of[stage].index(job)
        if stage == "mid":
            return b * len(of["mid"]) + (before - len(of["mid"]) + n)
        return before + n

    def job_no(stage, b, name, n=0):
        return number(stage, b, (name, n), {j[0] for jobs in JOBS.values() for j in jobs})

    def act_no(stage, b, name, n=0):
        return number(stage, b, (name, n), BY_ACT)

    def slot_of(stage, name, n=0):
        return JOBS[stage].index((name, n)) % 2

    with ExitStack() as stack:
        def sb(name, shape, dt=F32):
            return stack.enter_context(nc.sbuf_tensor(name, shape, dt))

        def sem(name):
            return stack.enter_context(nc.semaphore(name))

        ident = sb("ident", [P, P])
        raw = sb("raw", [P, NT, D])
        CT = 3
        ctxT_h = sb("ctxT_h", [P, CT, LK], F32R)
        ctxT_l = sb("ctxT_l", [P, CT, LK], F32R)
        NR = 4
        val_h = sb("val_h", [P, NR, BANK], F32R)
        val_l = sb("val_l", [P, NR, BANK], F32R)
        nT_h = sb("nT_h", [P, KD, LQ], F32R)
        nT_l = sb("nT_l", [P, KD, LQ], F32R)
        xn = sb("xn", [QT, NQ, D])
        x2 = sb("x2", [QT, NQ, D])
        xT_st = sb("xT_st", [P, KD, LQ])
        ar_h = sb("ar_h", [P, KD, RE], F32R)
        ar_l = sb("ar_l", [P, KD, RE], F32R)
        gated = sb("gated", [QT, NQ, G])
        gT_st = sb("gT_st", [P, KG, LQ])
        prob = sb("prob", [QT, NQ, NT * P])
        eT_h = sb("eT_h", [P, NQ, NT, QT], F32R)
        eT_l = sb("eT_l", [P, NQ, NT, QT], F32R)
        hT = sb("hT", [RE, LQ])
        hn = sb("hn", [QT, NQ, RE])
        st1 = sb("st1", [QT, NQ, CH, STATS])
        st2 = sb("st2", [QT, NQ, CH, STATS])
        mv1 = sb("mv1", [QT, NQ, 2])
        mv2 = sb("mv2", [QT, NQ, 2])
        ve1 = sb("ve1", [QT, NQ])
        ve2 = sb("ve2", [QT, NQ])
        rs1 = sb("rs1", [QT, NQ])
        rs2 = sb("rs2", [QT, NQ])
        nb1 = sb("nb1", [QT, NQ])
        nb2 = sb("nb2", [QT, NQ])
        mhalf = sb("mhalf", [QT, NQ])
        nmax = sb("nmax", [QT, NQ])
        rsum = sb("rsum", [QT, NQ])
        rinv = sb("rinv", [QT, NQ])
        rank = sb("rank", [QT, E])
        t16 = [sb(f"t16_{i}", [QT, NQ, E]) for i in range(10)]
        t1 = [sb(f"t1_{i}", [QT, NQ]) for i in range(9)]

        scores = stack.enter_context(nc.psum_tensor("scores", [P, NQ, 2 * BANK], F32))
        work = stack.enter_context(nc.psum_tensor("work", [P, 2, 2 * BANK], F32))

        ident_ready = sem("ident_ready")
        consts_ready = sem("consts_ready")
        ar_loaded = sem("ar_loaded")
        raw_loaded = [sem(f"raw_loaded{c}") for c in range(CH)]
        xn_loaded = sem("xn_loaded")
        xres_loaded = sem("xres_loaded")
        filled = sem("filled")
        high_done = sem("high_done")
        drained = sem("drained")
        score_step = sem("score_step")
        scores_done = sem("scores_done")
        max_ready = sem("max_ready")
        exp_done = sem("exp_done")
        rinv_ready = sem("rinv_ready")
        val_high = sem("val_high")
        val_ready = sem("val_ready")
        val_used = sem("val_used")
        pv_done = sem("pv_done")
        x2_done = sem("x2_done")
        x2_stored = sem("x2_stored")
        stat1, aggr1, var1, rstd1, bias1 = (sem(f"ln1_{n}") for n in ("stats", "aggr", "var", "rstd", "bias"))
        stat2, aggr2, var2, rstd2, bias2 = (sem(f"ln2_{n}") for n in ("stats", "aggr", "var", "rstd", "bias"))
        ln1_done = sem("ln1_done")
        ln2_done = sem("ln2_done")
        xT_staged = sem("xT_staged")
        xT_stored = sem("xT_stored")
        gT_stored = sem("gT_stored")
        route = sem("route")
        rexp_done = sem("rexp_done")
        gated_done = sem("gated_done")

        block = stack.enter_context(nc.Block())

        @block.sync
        def _(sp):
            def load_raw(b, c):
                cols = slice(c * BANK, (c + 1) * BANK)
                sp.dma_start(raw[:, 0:FULL, cols],
                             ctx[b, 0:FULL * P, cols].rearrange("(t p) d -> p t d", p=P)).then_inc(raw_loaded[c], 16)
                sp.dma_start(raw[0:REST, FULL, cols], ctx[b, FULL * P:LK, cols]).then_inc(raw_loaded[c], 16)

            def one(b, stage):
                last = stage == "last"
                if not last:
                    if stage == "first":
                        sp.wait_ge(filled, job_no("pre", 0, "qT", NX - 1) + 1)
                    else:
                        sp.wait_ge(filled, job_no("mid", b, "ctxT", 0))
                    sp.dma_start(xn[:, :, :], x_v[b + 1]).then_inc(xn_loaded, 16)
                if stage != "first":
                    sp.wait_ge(filled, job_no(stage, b, "x2T", NX - 1) + 1)
                sp.dma_start(x2[:, :, :], x_v[b]).then_inc(xres_loaded, 16)
                for c in range(CH):
                    if not last:
                        sp.wait_ge(val_ready, b * (CH * NT) + (c + 1) * NT)
                        load_raw(b + 1, c)
                    if stage != "first" and c == 0:
                        store_xT(b - 1)
                if stage != "first":
                    store_gT(b - 1, drained_gT=job_no(stage, b, "gT", NG - 1) + 1)
                sp.wait_ge(x2_done, (b + 1) * (NQ * CH))
                sp.dma_start(x2_v[b], x2[:, :, :]).then_inc(x2_stored, 16)

            def store_xT(b):
                sp.wait_ge(xT_staged, (b + 1) * NX)
                sp.dma_start(xT_d[:, :, bass.ds(b * LQ, LQ)], xT_st[:, :, :]).then_inc(xT_stored, 16)

            def store_gT(b, drained_gT):
                sp.wait_ge(drained, drained_gT)
                sp.dma_start(gT_d[:, :, bass.ds(b * LQ, LQ)], gT_st[:, :, :]).then_inc(gT_stored, 16)

            sp.dma_start(xn[:, :, :], x_v[0]).then_inc(xn_loaded, 16)
            an = gated[0:RE, :, :].rearrange("p q g -> p (q g)")
            sp.dma_start(an[0:R, :], A).then_inc(ar_loaded, 16)
            sp.dma_start(an[R:RE, :], router).then_inc(ar_loaded, 16)
            sp.wait_ge(consts_ready, 1)
            for c in range(CH):
                load_raw(0, c)
            one(0, "first")
            with sp.Fori(1, NB - 1) as b:
                one(b, "mid")
            one(NB - 1, "last")
            store_xT(NB - 1)
            store_gT(NB - 1, drained_gT=job_no("tail", NB, "gT", NG - 1) + 1)
            sp.wait_ge(x2_stored, NB * 16)
            sp.wait_ge(xT_stored, NB * 16)
            sp.wait_ge(gT_stored, NB * 16)

        @block.tensor
        def _(pe):
            def take(no):
                at_least(pe, drained, no - 1)

            def scores_of(b, stage):
                job = lambda k: job_no(stage, b, "ctxT", k)

                def transpose_block(k):
                    if k % (KD // CH) == 0:
                        pe.wait_ge(raw_loaded[k // (KD // CH)], b * 32 + 32)
                    take(job(k))
                    slot = slot_of(stage, "ctxT", k)
                    for t in range(NT):
                        rows = P if t < FULL else REST
                        last = pe.transpose(work[:, slot, t * P:t * P + rows],
                                            raw[0:rows, t, k * P:(k + 1) * P], ident[0:rows, 0:rows])
                    last.then_inc(filled, 1)

                transpose_block(0)
                transpose_block(1)
                if stage != "first":
                    pe.wait_ge(x2_done, b * (NQ * CH))
                def products(k, q):
                    for lo, hi in ((0, BANK), (BANK, LK)):
                        out = scores[0:QT, q, lo:hi]
                        qh = nT_h[:, k, q * QT:(q + 1) * QT]
                        ql = nT_l[:, k, q * QT:(q + 1) * QT]
                        ch = ctxT_h[:, k % CT, lo:hi]
                        cl = ctxT_l[:, k % CT, lo:hi]
                        pe.matmul(out, qh, ch, start=(k == 0), stop=False)
                        pe.matmul(out, qh, cl, start=False, stop=False)
                        last = pe.matmul(out, ql, ch, start=False, stop=(k == KD - 1))
                    return last

                for k in range(KD - 2):
                    transpose_block(k + 2)
                    pe.wait_ge(drained, job(k) + 1)
                    for q in range(NQ):
                        last = products(k, q)
                    last.then_inc(score_step, 1)
                for q in range(NQ):
                    for k in (KD - 2, KD - 1):
                        pe.wait_ge(drained, job(k) + 1)
                        last = products(k, q)
                    last.then_inc(scores_done, 1)

            def transpose_rows(stage, b, name, src, n):
                take(job_no(stage, b, name, n))
                slot = slot_of(stage, name, n)
                for i in range(4):
                    k = 4 * n + i
                    for q in range(NQ):
                        at = (i // 2) * BANK + (i % 2) * LQ + q * QT
                        last = pe.transpose(work[:, slot, at:at + QT],
                                            src[:, q, k * P:(k + 1) * P], ident[0:QT, 0:QT])
                last.then_inc(filled, 1)

            def hidden_of(stage, b):
                take(job_no(stage, b, "hid"))
                out = work[0:RE, slot_of(stage, "hid"), 0:LQ]
                for k in range(KD):
                    if k % 4 == 0:
                        pe.wait_ge(drained, job_no(stage, b, "x2T", k // 4) + 1)
                    pe.matmul(out, ar_h[:, k, :], nT_h[:, k, :], start=(k == 0), stop=False)
                    pe.matmul(out, ar_h[:, k, :], nT_l[:, k, :], start=False, stop=False)
                    last = pe.matmul(out, ar_l[:, k, :], nT_h[:, k, :], start=False, stop=(k == KD - 1))
                last.then_inc(filled, 1)

            def x2T_of(stage, b, of, src):
                pe.wait_ge(ln2_done, (of + 1) * NQ)
                for n in range(NX):
                    transpose_rows(stage, b, "x2T", src, n)

            def hidden_back(stage, b):
                take(job_no(stage, b, "hN"))
                pe.wait_ge(drained, job_no(stage, b, "hid") + 1)
                slot = slot_of(stage, "hN")
                for q in range(NQ):
                    last = pe.transpose(work[0:QT, slot, q * RE:(q + 1) * RE],
                                        hT[:, q * QT:(q + 1) * QT], ident[0:RE, 0:RE])
                last.then_inc(filled, 1)

            def exps_T(stage, b):
                for q in range(NQ):
                    pe.wait_ge(exp_done, b * NQ + q + 1)
                    take(job_no(stage, b, "eT", q))
                    slot = slot_of(stage, "eT", q)
                    for t in range(NT):
                        at = (t // 3) * BANK + (t % 3) * QT
                        last = pe.transpose(work[:, slot, at:at + QT],
                                            prob[:, q, t * P:(t + 1) * P], ident[0:QT, 0:QT])
                    last.then_inc(filled, 1)

            def outputs_of(stage, b):
                pe.wait_ge(drained, job_no(stage, b, "eT", NQ - 1) + 1)
                for e in range(CH * NT):
                    c, t = e // NT, e % NT
                    if stage != "first":
                        if e == HN_AT:
                            hidden_back(stage, b)
                        if e in GT_AT:
                            pe.wait_ge(gated_done, b * NQ)
                            transpose_rows(stage, b, "gT", gated, GT_AT.index(e))
                    if stage != "last" and e in QT_AT:
                        pe.wait_ge(ln1_done, b * NQ + 2 * NQ)
                        transpose_rows(stage, b, "qT", xn, QT_AT.index(e))
                    if t == 0 and c >= 2:
                        pe.wait_ge(x2_done, b * (NQ * CH) + NQ * (c - 1))
                    pe.wait_ge(val_ready, b * (CH * NT) + e + 1)
                    for q in range(NQ):
                        out = scores[0:QT, c % 2, q * BANK:(q + 1) * BANK]
                        eh, el = eT_h[:, q, t, :], eT_l[:, q, t, :]
                        vh, vl = val_h[:, e % NR, :], val_l[:, e % NR, :]
                        pe.matmul(out, eh, vh, start=(t == 0), stop=False)
                        pe.matmul(out, eh, vl, start=False, stop=False)
                        last = pe.matmul(out, el, vh, start=False, stop=(t == NT - 1))
                    last.then_inc(val_used, 1)

            def one(b, stage):
                scores_of(b, stage)
                if stage != "first":
                    x2T_of(stage, b, b - 1, x2)
                exps_T(stage, b)
                if stage != "first":
                    hidden_of(stage, b)
                outputs_of(stage, b)

            pe.wait_ge(ident_ready, 2)
            pe.wait_ge(ar_loaded, 32)
            an = gated[0:RE, :, :].rearrange("p q g -> p (q g)")
            for n in range(2):
                for i in range(8):
                    k = 8 * n + i
                    at = (i // 4) * BANK + (i % 4) * RE
                    last = pe.transpose(work[:, n, at:at + RE], an[:, k * P:(k + 1) * P], ident[0:RE, 0:RE])
                last.then_inc(filled, 1)
            pe.wait_ge(ln1_done, NQ)
            for n in range(NX):
                transpose_rows("pre", 0, "qT", xn, n)
            one(0, "first")
            with pe.Fori(1, NB - 1) as b:
                one(b, "mid")
            one(NB - 1, "last")
            x2T_of("tail", NB, NB - 1, xn)
            hidden_of("tail", NB)
            hidden_back("tail", NB)
            pe.wait_ge(gated_done, NB * NQ)
            for n in range(NG):
                transpose_rows("tail", NB, "gT", gated, n)

        @block.scalar
        def _(act):
            def high(stage, b, name, n, out, cols, width):
                act.wait_ge(filled, job_no(stage, b, name, n) + 1)
                src = work[:, slot_of(stage, name, n), :].rearrange("p (k c) -> p k c", k=cols)[:, :, 0:width]
                act.activation(out, src, ACT.Copy).then_inc(high_done, 1)

            def ctx_high(stage, b, k):
                if k >= CT:
                    act.wait_ge(score_step, b * (KD - 2) + k - CT + 1)
                act.wait_ge(filled, job_no(stage, b, "ctxT", k) + 1)
                act.activation(ctxT_h[:, k % CT, :], work[:, slot_of(stage, "ctxT", k), 0:LK],
                               ACT.Copy).then_inc(high_done, 1)

            def four_blocks(tile, n):
                return tile[:, 4 * n:4 * n + 4, :].rearrange("p (k i) c -> p k (i c)", k=2)

            def normalise(out, tile, q, rstd, bias, sem_done):
                act.activation(out[:, q, :], tile[:, q, :], ACT.Identity, bias=bias[:, q:q + 1],
                               scale=rstd[:, q:q + 1]).then_inc(sem_done, 1)

            def value_high(b, e):
                at_least(act, val_used, b * (CH * NT) + e - NR + 1)
                c, t = e // NT, e % NT
                act.activation(val_h[:, e % NR, :], raw[:, t, c * BANK:(c + 1) * BANK],
                               ACT.Copy).then_inc(val_high, 1)

            def exponentials(b, q):
                act.wait_ge(max_ready, b * NQ + q + 1)
                act.activation(prob[:, q, 0:LK], scores[0:QT, q, 0:LK], ACT.Exp, bias=nmax[:, q:q + 1],
                               scale=1.0, accum_out=rsum[:, q:q + 1]).then_inc(exp_done, 1)

            def routing_exp(of):
                act.wait_ge(route, of * ROUTE + 2)
                act.activation(t16[1][:, :, :], t16[0][:, :, :], ACT.Exp).then_inc(rexp_done, 1)

            def one(b, stage):
                for k in range(KD):
                    ctx_high(stage, b, k)
                    if stage != "first" and k in (7, 9):
                        if k == 7:
                            act.wait_ge(bias2, b)
                            act.wait_ge(x2_stored, b * 16)
                        normalise(x2, x2, (k - 7) // 2, rs2, nb2, ln2_done)
                    if k in (5, 8, 10, 11):
                        value_high(b, (5, 8, 10, 11).index(k))
                    if stage != "last" and k in (12, 14):
                        if k == 12:
                            act.wait_ge(bias1, b + 2)
                        normalise(xn, xn, (k - 12) // 2, rs1, nb1, ln1_done)
                x2T_high = lambda n: high(stage, b, "x2T", n, four_blocks(nT_h, n), 2, 2 * LQ)
                exponentials(b, 0)
                if stage != "first":
                    x2T_high(0)
                exponentials(b, 1)
                if stage != "first":
                    for n in range(1, NX):
                        x2T_high(n)
                for q in range(NQ):
                    high(stage, b, "eT", q, eT_h[:, q, :, :].rearrange("p (k i) c -> p k (i c)", k=2), 2, 3 * QT)
                for e in range(NR, CH * NT):
                    value_high(b, e)
                    if stage != "first" and e == ROUTE_EXP_AT:
                        routing_exp(b - 1)
                    if stage != "last" and e - 3 in QT_AT:
                        n = QT_AT.index(e - 3)
                        if stage == "mid" and n == 0:
                            act.wait_ge(xT_staged, b * NX)
                        high(stage, b, "qT", n, four_blocks(nT_h, n), 2, 2 * LQ)

            for n in range(2):
                high("pre", 0, "arT", n, ar_h[:, 8 * n:8 * n + 8, :].rearrange("p (k i) c -> p k (i c)", k=2), 2, 4 * RE)
            act.wait_ge(bias1, 1)
            for q in range(NQ):
                normalise(xn, xn, q, rs1, nb1, ln1_done)
            for n in range(NX):
                high("pre", 0, "qT", n, four_blocks(nT_h, n), 2, 2 * LQ)
            one(0, "first")
            with act.Fori(1, NB - 1) as b:
                one(b, "mid")
            one(NB - 1, "last")
            act.wait_ge(bias2, NB)
            for q in range(NQ):
                normalise(xn, x2, q, rs2, nb2, ln2_done)
            for n in range(NX):
                high("tail", NB, "x2T", n, four_blocks(nT_h, n), 2, 2 * LQ)
            routing_exp(NB - 1)

        @block.vector
        def _(dve):
            def low(stage, b, name, n, high_part, low_part, cols, width):
                dve.wait_ge(high_done, act_no(stage, b, name, n) + 1)
                src = work[:, slot_of(stage, name, n), :].rearrange("p (k c) -> p k c", k=cols)[:, :, 0:width]
                dve.tensor_tensor(low_part, src, as_f32(high_part), ALU.subtract).then_inc(drained, 1)

            def ctx_low(stage, b, k):
                dve.wait_ge(high_done, act_no(stage, b, "ctxT", k) + 1)
                dve.tensor_tensor(ctxT_l[:, k % CT, :], work[:, slot_of(stage, "ctxT", k), 0:LK],
                                  as_f32(ctxT_h[:, k % CT, :]), ALU.subtract).then_inc(drained, 1)

            def four_blocks(tile, n):
                return tile[:, 4 * n:4 * n + 4, :].rearrange("p (k i) c -> p k (i c)", k=2)

            def value_low(b, e):
                c, t = e // NT, e % NT
                dve.wait_ge(val_high, b * (CH * NT) + e + 1)
                dve.tensor_tensor(val_l[:, e % NR, :], raw[:, t, c * BANK:(c + 1) * BANK],
                                  as_f32(val_h[:, e % NR, :]), ALU.subtract).then_inc(val_ready, 1)

            def stats(tile, st, sem_stat, i):
                q, c = i // CH, i % CH
                dve.bn_stats(st[:, q, c, :], tile[:, q, c * BANK:(c + 1) * BANK]).then_inc(sem_stat, 1)

            def aggregate(st, mv, sem_aggr):
                for q in range(NQ):
                    dve.bn_aggr(mv[:, q, :], st[:, q, :, :].rearrange("p c s -> p (c s)")).then_inc(sem_aggr, 1)

            def variance(mv, ve, sem_aggr, sem_var, n):
                dve.wait_ge(sem_aggr, n * NQ + NQ)
                dve.tensor_scalar(ve[:, :], mv[:, :, 1], EPS, None, ALU.add).then_inc(sem_var, 1)

            def shift(mv, rs, nb, sem_rstd, sem_bias, n):
                dve.wait_ge(sem_rstd, n + 1)
                dve.scalar_tensor_tensor(nb[:, :], mv[:, :, 0], -1.0, rs[:, :], ALU.mult,
                                         ALU.mult).then_inc(sem_bias, 1)

            def row_max(b):
                for q in range(NQ):
                    dve.wait_ge(scores_done, b * NQ + q + 1)
                    dve.reduce_max(nmax[:, q:q + 1], scores[0:QT, q, 0:LK], AX.X,
                                   negate=True).then_inc(max_ready, 1)

            def residual(b, c):
                if c == 0:
                    dve.wait_ge(exp_done, b * NQ + NQ)
                    dve.reciprocal(rinv[:, :], rsum[:, :]).then_inc(rinv_ready, 1)
                    dve.wait_ge(xres_loaded, b * 16 + 16)
                    dve.wait_ge(rinv_ready, b + 1)
                dve.wait_ge(val_used, b * (CH * NT) + (c + 1) * NT)
                for q in range(NQ):
                    cols = slice(c * BANK, (c + 1) * BANK)
                    dve.scalar_tensor_tensor(x2[:, q, cols], scores[0:QT, c % 2, q * BANK:(q + 1) * BANK],
                                             rinv[:, q:q + 1], x2[:, q, cols], ALU.mult,
                                             ALU.add).then_inc(x2_done, 1)

            def hidden_out(stage, b):
                dve.wait_ge(filled, job_no(stage, b, "hid") + 1)
                dve.tensor_copy(hT[:, :], work[0:RE, slot_of(stage, "hid"), 0:LQ]).then_inc(drained, 1)

            def hidden_back(stage, b):
                dve.wait_ge(filled, job_no(stage, b, "hN") + 1)
                dve.tensor_copy(hn[:, :, :].rearrange("p q r -> p (q r)"),
                                work[0:QT, slot_of(stage, "hN"), 0:NQ * RE]).then_inc(drained, 1)

            def wide(v):
                return v.unsqueeze(2).to_broadcast([QT, NQ, E])

            rank_w = rank[:, :].unsqueeze(1).to_broadcast([QT, NQ, E])

            def route_steps(stage, b, of):
                logits = hn[:, :, R:RE]
                z, ez, p, eq1, key1, one1, p_rest, eq2, key2, one2 = (t[:, :, :] for t in t16)
                lmax, s, rs, m1, k1, m2, k2, den, rden = (t[:, :] for t in t1)
                v = dve
                return [
                    lambda: v.reduce_max(lmax, logits, AX.X),
                    lambda: v.tensor_tensor(z, logits, wide(lmax), ALU.subtract),
                    lambda: v.reduce_sum(s, ez, AX.X),
                    lambda: v.reciprocal(rs, s),
                    lambda: v.tensor_tensor(p, ez, wide(rs), ALU.mult),
                    lambda: v.reduce_max(m1, p, AX.X),
                    lambda: v.tensor_tensor(eq1, p, wide(m1), ALU.is_equal),
                    lambda: v.tensor_tensor(key1, eq1, rank_w, ALU.mult),
                    lambda: v.reduce_max(k1, key1, AX.X),
                    lambda: v.tensor_tensor(one1, key1, wide(k1), ALU.is_equal),
                    lambda: v.scalar_tensor_tensor(p_rest, one1, -2.0, p, ALU.mult, ALU.add),
                    lambda: v.reduce_max(m2, p_rest, AX.X),
                    lambda: v.tensor_tensor(eq2, p_rest, wide(m2), ALU.is_equal),
                    lambda: v.tensor_tensor(key2, eq2, rank_w, ALU.mult),
                    lambda: v.reduce_max(k2, key2, AX.X),
                    lambda: v.tensor_tensor(one2, key2, wide(k2), ALU.is_equal),
                    lambda: v.tensor_tensor(one1, one1, one2, ALU.add),
                    lambda: v.tensor_tensor(den, m1, m2, ALU.add),
                    lambda: v.tensor_scalar(den, den, TOP_EPS, 1.0 / SCALING, ALU.add, ALU.mult),
                    lambda: v.reciprocal(rden, den),
                    lambda: v.tensor_tensor(z, one1, p, ALU.mult),
                    lambda: v.tensor_tensor(ez, z, wide(rden), ALU.mult),
                ]

            def run_route(stage, b, of, lo, hi):
                steps = route_steps(stage, b, of)
                assert len(steps) == ROUTE
                for n in range(lo, hi):
                    if n == 0:
                        dve.wait_ge(drained, job_no(stage, b, "hN") + 1)
                    else:
                        dve.wait_ge(route, of * ROUTE + n)
                    if n == 2:
                        dve.wait_ge(rexp_done, of + 1)
                    steps[n]().then_inc(route, 1)

            def gated_T(stage, b, of, n):
                if n == 0:
                    at_least(dve, gT_stored, of * 16)
                dve.wait_ge(filled, job_no(stage, b, "gT", n) + 1)
                src = work[:, slot_of(stage, "gT", n), :].rearrange("p (k c) -> p k c", k=2)[:, :, 0:2 * LQ]
                dve.tensor_copy(four_blocks(gT_st, n), src).then_inc(drained, 1)

            def one(b, stage):
                old, new = stage != "first", stage != "last"
                for k in range(KD):
                    ctx_low(stage, b, k)
                    if old and k < 4:
                        if k == 0:
                            dve.wait_ge(x2_done, b * (NQ * CH))
                        stats(x2, st2, stat2, 2 * k)
                        stats(x2, st2, stat2, 2 * k + 1)
                        if k == 3:
                            dve.wait_ge(stat2, b * (NQ * CH))
                    if old and k == 4:
                        aggregate(st2, mv2, aggr2)
                        variance(mv2, ve2, aggr2, var2, b - 1)
                    if old and k == 5:
                        shift(mv2, rs2, nb2, rstd2, bias2, b - 1)
                    if new and 6 <= k < 10:
                        if k == 6:
                            dve.wait_ge(xn_loaded, b * 16 + 32)
                        stats(xn, st1, stat1, 2 * (k - 6))
                        stats(xn, st1, stat1, 2 * (k - 6) + 1)
                        if k == 9:
                            dve.wait_ge(stat1, b * (NQ * CH) + 2 * NQ * CH)
                    if new and k == 10:
                        aggregate(st1, mv1, aggr1)
                        variance(mv1, ve1, aggr1, var1, b + 1)
                    if new and k == 11:
                        shift(mv1, rs1, nb1, rstd1, bias1, b + 1)
                    if k in (11, 12, 13, 14):
                        value_low(b, k - 11)
                row_max(b)
                if old:
                    for n in range(NX):
                        low(stage, b, "x2T", n, four_blocks(nT_h, n), four_blocks(nT_l, n), 2, 2 * LQ)
                for q in range(NQ):
                    three = lambda tile: tile[:, q, :, :].rearrange("p (k i) c -> p k (i c)", k=2)
                    low(stage, b, "eT", q, three(eT_h), three(eT_l), 2, 3 * QT)
                if old:
                    hidden_out(stage, b)
                for e in range(NR, CH * NT):
                    value_low(b, e)
                    c, t = e // NT, e % NT
                    if old and e == HN_AT + 3:
                        hidden_back(stage, b)
                    if old and e in ROUTE_AT:
                        run_route(stage, b, b - 1, *ROUTE_AT[e])
                    if new and e - 3 in QT_AT:
                        n = QT_AT.index(e - 3)
                        low(stage, b, "qT", n, four_blocks(nT_h, n), four_blocks(nT_l, n), 2, 2 * LQ)
                    if old and e - 3 in GT_AT:
                        gated_T(stage, b, b - 1, GT_AT.index(e - 3))
                    if c >= 1 and t == 3:
                        residual(b, c - 1)
                residual(b, CH - 1)

            dve.memset(raw[96:P, FULL, :], 0.0).then_inc(consts_ready, 1)
            dve.memset(prob[:, :, LK:NT * P], 0.0).then_inc(consts_ready, 1)
            for e in range(E):
                dve.memset(rank[:, e:e + 1], float(E - e)).then_inc(consts_ready, 1)
            dve.wait_ge(xn_loaded, 16)
            for i in range(NQ * CH):
                stats(xn, st1, stat1, i)
            dve.wait_ge(stat1, NQ * CH)
            aggregate(st1, mv1, aggr1)
            variance(mv1, ve1, aggr1, var1, 0)
            shift(mv1, rs1, nb1, rstd1, bias1, 0)
            for n in range(2):
                eight = lambda tile: tile[:, 8 * n:8 * n + 8, :].rearrange("p (k i) c -> p k (i c)", k=2)
                low("pre", 0, "arT", n, eight(ar_h), eight(ar_l), 2, 4 * RE)
            for n in range(NX):
                low("pre", 0, "qT", n, four_blocks(nT_h, n), four_blocks(nT_l, n), 2, 2 * LQ)
            dve.wait_ge(consts_ready, 2 + E)
            one(0, "first")
            with dve.Fori(1, NB - 1) as b:
                one(b, "mid")
            one(NB - 1, "last")
            dve.wait_ge(x2_done, NB * NQ * CH)
            for i in range(NQ * CH):
                stats(x2, st2, stat2, i)
            dve.wait_ge(stat2, NB * NQ * CH)
            aggregate(st2, mv2, aggr2)
            variance(mv2, ve2, aggr2, var2, NB - 1)
            shift(mv2, rs2, nb2, rstd2, bias2, NB - 1)
            for n in range(NX):
                low("tail", NB, "x2T", n, four_blocks(nT_h, n), four_blocks(nT_l, n), 2, 2 * LQ)
            hidden_out("tail", NB)
            hidden_back("tail", NB)
            run_route("tail", NB, NB - 1, 0, ROUTE)
            for n in range(NG):
                gated_T("tail", NB, NB - 1, n)

        @block.gpsimd
        def _(pool):
            def reciprocal_root(ve, rs, sem_var, sem_rstd, n):
                pool.wait_ge(sem_var, n + 1)
                pool.tensor_tensor(rs[:, :], ve[:, :], mhalf[:, :], ALU.pow).then_inc(sem_rstd, 1)

            def stage_xT(stage, b, of):
                if not (isinstance(of, int) and of == 0):
                    at_least(pool, xT_stored, of * 16)
                for n in range(NX):
                    pool.wait_ge(drained, job_no(stage, b, "x2T", n) + 1)
                    cut = slice(4 * n, 4 * n + 4)
                    pool.tensor_tensor(xT_st[:, cut, :], as_f32(nT_h[:, cut, :]), as_f32(nT_l[:, cut, :]),
                                       ALU.add).then_inc(xT_staged, 1)

            def gate(of):
                pool.wait_ge(route, of * ROUTE + ROUTE)
                for q in range(NQ):
                    pool.tensor_tensor(gated[:, q, :].rearrange("p (e r) -> p e r", e=E),
                                       t16[1][:, q, :].unsqueeze(2).to_broadcast([QT, E, R]),
                                       hn[:, q, 0:R].unsqueeze(1).to_broadcast([QT, E, R]),
                                       ALU.mult).then_inc(gated_done, 1)

            build_identity(pool, ident, ident_ready)
            pool.memset(mhalf[:, :], -0.5).then_inc(ident_ready, 1)
            pool.wait_ge(ident_ready, 3)
            reciprocal_root(ve1, rs1, var1, rstd1, 0)
            reciprocal_root(ve1, rs1, var1, rstd1, 1)
            with pool.Fori(1, NB - 1) as b:
                reciprocal_root(ve2, rs2, var2, rstd2, b - 1)
                reciprocal_root(ve1, rs1, var1, rstd1, b + 1)
                stage_xT("mid", b, b - 1)
                gate(b - 1)
            reciprocal_root(ve2, rs2, var2, rstd2, NB - 2)
            stage_xT("last", NB - 1, NB - 2)
            gate(NB - 2)
            reciprocal_root(ve2, rs2, var2, rstd2, NB - 1)
            stage_xT("tail", NB, NB - 1)
            gate(NB - 1)


ROUTE = 22
HN_AT = 2
QT_AT = (8, 10, 12, 14)
GT_AT = (18, 20)
ROUTE_EXP_AT = 7
ROUTE_AT = {6: (0, 2), 8: (2, 5), 9: (5, 8), 10: (8, 11), 12: (11, 14), 13: (14, 17), 14: (17, 20), 15: (20, ROUTE)}


def linear_phase(nc, W, bias, Bw, x2_d, xT_d, gT_d, out):
    D = W.shape[0]
    E, _, R = Bw.shape
    T = out.shape[0]
    NT = T // P
    KW = W.shape[1] // P
    KG = E * R // P
    K = KW + KG
    NC = D // BANK
    OT = BANK // P
    PK = 4
    NP = K // PK
    WP = KW // PK
    RING = 3
    EP = PK * P // R
    PSR = 4
    assert T % P == 0 and NT % 2 == 0 and NP % RING == 0 and K % PSR == 0

    with ExitStack() as stack:
        def sb(name, shape, dt=F32):
            return stack.enter_context(nc.sbuf_tensor(name, shape, dt))

        def sem(name):
            return stack.enter_context(nc.semaphore(name))

        ident = sb("ident2", [P, P])
        w_h = sb("w_h", [P, K, BANK], F32R)
        w_l = sb("w_l", [P, K, BANK], F32R)
        piece = sb("piece", [P, RING, OT, PK * P])
        a_raw = sb("a_raw", [P, K, P])
        a_h = sb("a_h", [P, 2, K, P], F32R)
        a_l = sb("a_l", [P, 2, K, P], F32R)
        res = sb("res", [P, 2, BANK])
        bias_b = sb("bias_b", [P, BANK])

        acc = stack.enter_context(nc.psum_tensor("acc", [P, 2, BANK], F32))
        wT = stack.enter_context(nc.psum_tensor("wT", [P, PSR, BANK], F32))

        ident_ready = sem("ident2_ready")
        piece_loaded = [sem(f"piece_loaded{s}") for s in range(RING)]
        w_filled = sem("w_filled")
        w_high = sem("w_high")
        w_ready = sem("w_ready")
        ax_loaded = sem("ax_loaded")
        ag_loaded = sem("ag_loaded")
        ax_high = sem("ax_high")
        ag_high = sem("ag_high")
        ax_low = sem("ax_low")
        ag_low = sem("ag_low")
        res_loaded = [sem(f"res_loaded{i}") for i in range(2)]
        bias_loaded = sem("bias_loaded")
        res_ready = sem("res_ready")
        tile_done = sem("tile_done")
        out_ready = sem("out_ready")
        out_stored = [sem(f"out_stored{i}") for i in range(2)]

        LOADS = [1 if p < WP else OT for p in range(NP)]

        def piece_count(c, p):
            mine = [j for j in range(NP) if j % RING == p % RING]
            total = 16 * sum(LOADS[j] for j in mine)
            return c * total + 16 * sum(LOADS[j] for j in mine if j <= p)

        def load_piece(eng, c, p):
            s = p % RING
            if p < WP:
                src = W[bass.ds(c * BANK, BANK), p * PK * P:(p + 1) * PK * P].rearrange("(o p) i -> p o i", p=P)
                eng.dma_start(piece[:, s, :, :], src).then_inc(piece_loaded[s], 16)
            else:
                for o in range(OT):
                    e0 = (p - WP) * EP
                    src = Bw[e0:e0 + EP, bass.ds(c * BANK + o * P, P), :].rearrange("e p r -> p e r")
                    dst = piece[:, s, o, :].rearrange("p (e r) -> p e r", e=EP)
                    eng.dma_start(dst, src).then_inc(piece_loaded[s], 16)

        block = stack.enter_context(nc.Block())

        @block.sync
        def _(sp):
            def load_tile(c, t, par):
                g = c * NT + t
                at_least(sp, ax_low, g)
                sp.dma_start(a_raw[:, 0:KW, :], xT_d[:, :, bass.ds(t * P, P)]).then_inc(ax_loaded, 16)
                at_least(sp, ag_low, g)
                sp.dma_start(a_raw[:, KW:K, :], gT_d[:, :, bass.ds(t * P, P)]).then_inc(ag_loaded, 16)

            def load_res(c, t, par, half):
                at_least(sp, out_stored[par], half * 16)
                sp.dma_start(res[:, par, :], x2_d[bass.ds(t * P, P), bass.ds(c * BANK, BANK)]).then_inc(
                    res_loaded[par], 16)

            def load_bias(c):
                at_least(sp, res_ready, c * NT)
                sp.dma_start(bias_b[:, :], bias[bass.ds(c * BANK, BANK)].unsqueeze(0).to_broadcast([P, BANK])
                             ).then_inc(bias_loaded, 16)

            def pair(c, i):
                for par in range(2):
                    load_tile(c, i * 2 + par, par)
                    load_res(c, i * 2 + par, par, c * (NT // 2) + i)

            def chunk(c):
                load_bias(c)
                if isinstance(c, int) and c == 0:
                    pair(c, 0)
                    with sp.Fori(1, NT // 2) as i:
                        pair(c, i)
                else:
                    with sp.Fori(0, NT // 2) as i:
                        pair(c, i)

            chunk(0)
            with sp.Fori(1, NC) as c:
                chunk(c)

        @block.tensor
        def _(pe):
            def transpose_weights(c, k):
                p, kk = k // PK, k % PK
                if kk == 0:
                    pe.wait_ge(piece_loaded[p % RING], piece_count(c, p))
                if not (isinstance(c, int) and c == 0 and k < PSR):
                    pe.wait_ge(w_ready, c * K + k - PSR + 1)
                for o in range(OT):
                    last = pe.transpose(wT[:, k % PSR, o * P:(o + 1) * P],
                                        piece[:, p % RING, o, kk * P:(kk + 1) * P], ident[:, :])
                last.then_inc(w_filled, 1)

            def block_products(c, k, par):
                out = acc[:, par, :]
                pe.matmul(out, a_h[:, par, k, :], w_h[:, k, :], start=(k == 0), stop=False)
                pe.matmul(out, a_h[:, par, k, :], w_l[:, k, :], start=False, stop=False)
                return pe.matmul(out, a_l[:, par, k, :], w_h[:, k, :], start=False, stop=(k == K - 1))

            def start_tile(g):
                if not isinstance(g, int) or g >= 2:
                    at_least(pe, out_ready, g - 1)
                pe.wait_ge(ax_low, g + 1)

            def tile(c, g, par, first=False):
                start_tile(g)
                for k in range(K):
                    if k == KW:
                        pe.wait_ge(ag_low, g + 1)
                    if first:
                        pe.wait_ge(w_ready, c * K + k + 1)
                    last = block_products(c, k, par)
                last.then_inc(tile_done, 1)

            def chunk(c, more):
                g0 = c * NT
                tile(c, g0, 0, first=True)
                tile(c, g0 + 1, 1)
                with pe.Fori(1, NT // 2 - 1) as i:
                    tile(c, g0 + i * 2, 0)
                    tile(c, g0 + i * 2 + 1, 1)
                tile(c, g0 + NT - 2, 0)
                if not more:
                    tile(c, g0 + NT - 1, 1)
                    return
                start_tile(g0 + NT - 1)
                for k in range(K):
                    if k == KW:
                        pe.wait_ge(ag_low, g0 + NT)
                    last = block_products(c, k, 1)
                    if k == K - 1:
                        last.then_inc(tile_done, 1)
                    transpose_weights(c + 1, k)

            pe.wait_ge(ident_ready, 2)
            for k in range(K):
                transpose_weights(0, k)
            chunk(0, True)
            with pe.Fori(1, NC - 1) as c:
                chunk(c, True)
            chunk(NC - 1, False)

        @block.scalar
        def _(act):
            def weight_high(c, k, next_too):
                act.wait_ge(w_filled, c * K + k + 1)
                act.activation(w_h[:, k, :], wT[:, k % PSR, :], ACT.Copy).then_inc(w_high, 1)
                if k % PK == PK - 1:
                    p = k // PK
                    if p + RING < NP:
                        load_piece(act, c, p + RING)
                    elif next_too:
                        load_piece(act, c + 1, p + RING - NP)

            def split_high(g, par):
                if not isinstance(g, int) or g >= 2:
                    at_least(act, tile_done, g - 1)
                act.wait_ge(ax_loaded, g * 16 + 16)
                act.activation(a_h[:, par, 0:KW, :], a_raw[:, 0:KW, :], ACT.Copy).then_inc(ax_high, 1)
                act.wait_ge(ag_loaded, g * 16 + 16)
                act.activation(a_h[:, par, KW:K, :], a_raw[:, KW:K, :], ACT.Copy).then_inc(ag_high, 1)

            def store(c, t, par):
                act.wait_ge(out_ready, c * NT + t + 1)
                act.dma_start(out[bass.ds(t * P, P), bass.ds(c * BANK, BANK)], res[:, par, :]).then_inc(
                    out_stored[par], 16)

            def chunk(c, first, more):
                g0 = c * NT
                if first:
                    split_high(g0 + 1, 1)
                    store(c, 0, 0)
                    split_high(g0 + 2, 0)
                    store(c, 1, 1)
                    lo = 1
                else:
                    lo = 0
                with act.Fori(lo, NT // 2 - 1) as i:
                    split_high(g0 + i * 2 + 1, 1)
                    store(c, i * 2, 0)
                    split_high(g0 + i * 2 + 2, 0)
                    store(c, i * 2 + 1, 1)
                split_high(g0 + NT - 1, 1)
                store(c, NT - 2, 0)
                if more:
                    split_high(g0 + NT, 0)
                    for k in range(K):
                        weight_high(c + 1, k, next_too=not (isinstance(c, int) and c == NC - 2))
                store(c, NT - 1, 1)

            for p in range(RING):
                load_piece(act, 0, p)
            split_high(0, 0)
            for k in range(K):
                weight_high(0, k, True)
            chunk(0, True, True)
            with act.Fori(1, NC - 2) as c:
                chunk(c, False, True)
            chunk(NC - 2, False, True)
            chunk(NC - 1, False, False)
            for par in range(2):
                act.wait_ge(out_stored[par], NC * (NT // 2) * 16)

        @block.vector
        def _(dve):
            def weight_low(c, k):
                dve.wait_ge(w_high, c * K + k + 1)
                dve.tensor_tensor(w_l[:, k, :], wT[:, k % PSR, :], as_f32(w_h[:, k, :]),
                                  ALU.subtract).then_inc(w_ready, 1)

            def split_low(g, par):
                dve.wait_ge(ax_high, g + 1)
                dve.tensor_tensor(a_l[:, par, 0:KW, :], a_raw[:, 0:KW, :], as_f32(a_h[:, par, 0:KW, :]),
                                  ALU.subtract).then_inc(ax_low, 1)

            def finish(g, par):
                dve.wait_ge(res_ready, g + 1)
                dve.wait_ge(tile_done, g + 1)
                dve.tensor_tensor(res[:, par, :], acc[:, par, :], res[:, par, :], ALU.add).then_inc(out_ready, 1)

            def chunk(c, more):
                g0 = c * NT
                with dve.Fori(0, NT // 2 - 1) as i:
                    split_low(g0 + i * 2 + 1, 1)
                    finish(g0 + i * 2, 0)
                    split_low(g0 + i * 2 + 2, 0)
                    finish(g0 + i * 2 + 1, 1)
                split_low(g0 + NT - 1, 1)
                finish(g0 + NT - 2, 0)
                if more:
                    split_low(g0 + NT, 0)
                    for k in range(K):
                        weight_low(c + 1, k)
                finish(g0 + NT - 1, 1)

            split_low(0, 0)
            for k in range(K):
                weight_low(0, k)
            with dve.Fori(0, NC - 1) as c:
                chunk(c, True)
            chunk(NC - 1, False)

        @block.gpsimd
        def _(pool):
            def tile(c, g, par, half):
                pool.wait_ge(ag_high, g + 1)
                pool.tensor_tensor(a_l[:, par, KW:K, :], a_raw[:, KW:K, :], as_f32(a_h[:, par, KW:K, :]),
                                   ALU.subtract).then_inc(ag_low, 1)
                pool.wait_ge(bias_loaded, c * 16 + 16)
                pool.wait_ge(res_loaded[par], half * 16 + 16)
                pool.tensor_tensor(res[:, par, :], res[:, par, :], bias_b[:, :], ALU.add).then_inc(res_ready, 1)

            build_identity(pool, ident, ident_ready)
            with pool.Fori(0, NC) as c:
                with pool.Fori(0, NT // 2) as i:
                    for par in range(2):
                        tile(c, c * NT + i * 2 + par, par, c * (NT // 2) + i)


def xattn_ffn_kernel(nc, x, ctx_4096, L0_ffn_base_w, L0_ffn_base_b, L0_ffn_A, L0_ffn_B, L0_ffn_router_w, out):
    NB, LQ, D = x.shape
    T = NB * LQ
    E, _, R = L0_ffn_B.shape
    x2_d = nc.dram_tensor("x2_scratch", [T, D], F32).ap()
    xT_d = nc.dram_tensor("xT_scratch", [P, D // P, T], F32).ap()
    gT_d = nc.dram_tensor("gT_scratch", [P, E * R // P, T], F32).ap()
    attention_phase(nc, x, ctx_4096, L0_ffn_A, L0_ffn_router_w, x2_d, xT_d, gT_d)
    linear_phase(nc, L0_ffn_base_w, L0_ffn_base_b, L0_ffn_B, x2_d, xT_d, gT_d,
                 out.rearrange("b s d -> (b s) d"))


_INS = ["x", "ctx_4096", "L0_ffn_base_w", "L0_ffn_base_b", "L0_ffn_A", "L0_ffn_B", "L0_ffn_router_w"]
_OUTS = [((8, 224, 2048), "float32")]


def kernel(**inputs):
    import numpy as _np
    import concourse.bacc as _bacc
    from concourse import mybir as _mybir
    from concourse.bass_utils import run_bass_kernel_spmd as _run

    nc = _bacc.Bacc("TRN2", target_bir_lowering=False, num_devices=1)
    arrays, args = {}, []
    for name in _INS:
        a = _np.ascontiguousarray(inputs[name])
        arrays[f"in_{name}_dram"] = a
        args.append(nc.dram_tensor(f"in_{name}_dram", a.shape, _mybir.dt.from_np(a.dtype), kind="ExternalInput").ap())
    for i, (shape, dtype) in enumerate(_OUTS):
        dt = _mybir.dt.from_np(_np.dtype(dtype))
        args.append(nc.dram_tensor(f"out_{i}_dram", shape, dt, kind="ExternalOutput").ap())
    xattn_ffn_kernel(nc, *args)
    r = _run(nc, [arrays], core_ids=[0])
    got = tuple(r.results[0][f"out_{i}_dram"] for i in range(len(_OUTS)))
    return got[0]
```

```python
from contextlib import ExitStack

import concourse.bass as bass
from concourse import mybir

ALU = mybir.AluOpType
ACT = mybir.ActivationFunctionType
AX = mybir.AxisListType
F32 = mybir.dt.float32
F32R = mybir.dt.float32r

P = 128
BANK = 512
EPS = 1e-5
TOP_EPS = 1e-6
SCALING = 0.5
STATS = 6


def as_f32(ap):
    return ap.bitcast(F32)


def at_least(eng, sem, value):
    if isinstance(value, int) and value <= 0:
        return
    eng.wait_ge(sem, value)


ROUTE = 22
HN_AT = 2
LN1_AT = (4, 6)
QT_AT = (8, 10, 12, 14)
GT_AT = (18, 20)
NEXT_AT = (21, 22)
FIRST_W_AT = (22, 23)
SPLIT_G_AT = 14
ROUTE_EXP_AT = 7
ROUTE_AT = {6: (0, 2), 8: (2, 5), 9: (5, 8), 10: (8, 11), 12: (11, 14), 13: (14, 17), 14: (17, 20), 15: (20, ROUTE)}


def build_identity(pool, ident, sem):
    pool.memset(ident[:, :], 0.0).then_inc(sem, 1)
    pool.wait_ge(sem, 1)
    pool.affine_select(out=ident[:, :], in_=ident[:, :], compare_op=ALU.not_equal, fill=1.0, base=0,
                       pattern=[[-1, P]], channel_multiplier=1).then_inc(sem, 1)


def xattn_ffn_kernel(nc, x, ctx, W, bias, A, Bw, router, out):
    NB, LQ, D = x.shape
    LK = ctx.shape[1]
    R, E = A.shape[0], router.shape[0]
    QT = LQ // 2
    NQ = 2
    KD = D // P
    NT = -(-LK // P)
    FULL = LK // P
    REST = LK - FULL * P
    CH = D // BANK
    RE = R + E
    G = R * E
    KG = G // P
    LOGITS = 16
    assert LQ == NQ * QT and D == CH * BANK and RE <= P and G % P == 0

    T = NB * LQ
    TT = T // P
    KB = KG
    KW = W.shape[1] // P
    K = KB + KW
    NC = D // BANK
    OT = BANK // P
    PK = 4
    NP = K // PK
    BP = KB // PK
    RING = 3
    XP = KW // 4
    EP = PK * P // R
    WB = 2
    assert T % P == 0 and TT % 2 == 0 and NP % RING == 0 and K % WB == 0 and D == W.shape[0]

    x2_d = nc.dram_tensor("x2_scratch", [T, D], F32).ap()
    xT_d = nc.dram_tensor("xT_scratch", [P, KD, T], F32).ap()
    gT_d = nc.dram_tensor("gT_scratch", [P, KG, T], F32).ap()
    out = out.rearrange("b s d -> (b s) d")
    x_v = x.rearrange("b (q p) d -> b p q d", p=QT)
    x2_v = x2_d.rearrange("(b q p) d -> b p q d", q=NQ, p=QT)

    NX = KD // 4
    NG = KG // 4
    def group(name, n):
        return [(name, i) for i in range(n)]
    X2T_AFTER = (KD - 3, KD - 2, KD - 1)
    BEFORE = [j for k in range(KD) for j in [("ctxT", k)] +
              ([("x2T", X2T_AFTER.index(k))] if k in X2T_AFTER else [])] + [("x2T", NX - 1)]
    HID_EARLY = KD - 7
    OLD = [("hid", 0), ("hN", 0)]
    JOBS = {
        "pre": group("qT", NX),
        "first": group("ctxT", KD) + group("eT", NQ) + group("qT", NX) + group("arT", 2),
        "mid": BEFORE + group("eT", NQ) + OLD + group("qT", NX) + group("gT", NG),
        "last": BEFORE + group("eT", NQ) + OLD + group("gT", NG),
        "tail": group("x2T", NX) + OLD + group("gT", NG),
    }
    BY_ACT = ("arT", "qT", "ctxT", "x2T", "eT")
    TIMES = {"pre": 1, "first": 1, "mid": NB - 2, "last": 1, "tail": 1}
    assert all(len(jobs) % 2 == 0 for jobs in JOBS.values())

    def number(stage, b, job, kinds):
        of = {name: [j for j in jobs if j[0] in kinds] for name, jobs in JOBS.items()}
        before = 0
        for name in JOBS:
            if name == stage:
                break
            before += TIMES[name] * len(of[name])
        n = of[stage].index(job)
        if stage == "mid":
            return b * len(of["mid"]) + (before - len(of["mid"]) + n)
        return before + n

    def job_no(stage, b, name, n=0):
        return number(stage, b, (name, n), {j[0] for jobs in JOBS.values() for j in jobs})

    def act_no(stage, b, name, n=0):
        return number(stage, b, (name, n), BY_ACT)

    def slot_of(stage, name, n=0):
        return JOBS[stage].index((name, n)) % 2

    with ExitStack() as stack:
        def sb(name, shape, dt=F32, of=stack):
            return of.enter_context(nc.sbuf_tensor(name, shape, dt))

        def sem(name):
            return stack.enter_context(nc.semaphore(name))

        ident = sb("ident", [P, P])
        gated = sb("gated", [QT, NQ, G])
        gT_st = sb("gT_st", [P, KG, LQ])
        hT = sb("hT", [RE, LQ])
        hn = sb("hn", [QT, NQ, RE])
        st1 = sb("st1", [QT, NQ, CH, STATS])
        st2 = sb("st2", [QT, NQ, CH, STATS])
        mv1 = sb("mv1", [QT, NQ, 2])
        mv2 = sb("mv2", [QT, NQ, 2])
        ve1 = sb("ve1", [QT, NQ])
        ve2 = sb("ve2", [QT, NQ])
        rs1 = sb("rs1", [QT, NQ])
        rs2 = sb("rs2", [QT, NQ])
        nb1 = sb("nb1", [QT, NQ])
        nb2 = sb("nb2", [QT, NQ])
        mhalf = sb("mhalf", [QT, NQ])
        nmax = sb("nmax", [QT, NQ])
        rsum = sb("rsum", [QT, NQ])
        rinv = sb("rinv", [QT, NQ])
        rank = sb("rank", [QT, E])
        t16 = [sb(f"t16_{i}", [QT, NQ, E]) for i in range(10)]
        t1 = [sb(f"t1_{i}", [QT, NQ]) for i in range(9)]

        CT = 3
        NR = 4
        with ExitStack() as first:
            ctxT_h = sb("ctxT_h", [P, CT, LK], F32R, first)
            ctxT_l = sb("ctxT_l", [P, CT, LK], F32R, first)
            prob = sb("prob", [QT, NQ, NT * P], F32, first)
            xn = sb("xn", [QT, NQ, D], F32, first)
            val_h = sb("val_h", [P, NR, BANK], F32R, first)
            val_l = sb("val_l", [P, NR, BANK], F32R, first)
            eT_h = sb("eT_h", [P, NQ, NT, QT], F32R, first)
            eT_l = sb("eT_l", [P, NQ, NT, QT], F32R, first)
            raw = sb("raw", [P, NT, D], F32, first)
            x2 = sb("x2", [QT, NQ, D], F32, first)
            nT_h = sb("nT_h", [P, KD, LQ], F32R, first)
            nT_l = sb("nT_l", [P, KD, LQ], F32R, first)
            xT_st = sb("xT_st", [P, KD, LQ], F32, first)
            ar_h = sb("ar_h", [P, KD, RE], F32R, first)
            ar_l = sb("ar_l", [P, KD, RE], F32R, first)

        ag_h, ag_l, ax_h, ax_l = ([None, None] for _ in range(4))
        ag_h[0] = sb("ag_h0", [P, KB, P], F32R)
        ag_l[0] = sb("ag_l0", [P, KB, P], F32R)
        a_raw = sb("a_raw", [P, K, P])
        piece = sb("piece", [P, RING, OT, PK * P])
        ax_h[0] = sb("ax_h0", [P, KW, P], F32R)
        ax_l[0] = sb("ax_l0", [P, KW, P], F32R)
        res = sb("res", [P, 2, BANK])
        bias_b = sb("bias_b", [P, BANK])
        sb("spacer", [P, 32])
        w_hl = sb("w_hl", [P, K, 2, BANK], F32R)
        ax_h[1] = sb("ax_h1", [P, KW, P], F32R)
        ax_l[1] = sb("ax_l1", [P, KW, P], F32R)
        ag_h[1] = sb("ag_h1", [P, KB, P], F32R)
        ag_l[1] = sb("ag_l1", [P, KB, P], F32R)

        def a_block(par, k):
            if k < KB:
                return ag_h[par][:, k, :], ag_l[par][:, k, :]
            return ax_h[par][:, k - KB, :], ax_l[par][:, k - KB, :]

        scores = stack.enter_context(nc.psum_tensor("scores", [P, NQ, 2 * BANK], F32))
        work = stack.enter_context(nc.psum_tensor("work", [P, 2, 2 * BANK], F32))
        def place(stage, name, n=0):
            if stage == "pre" and n >= 2:
                return scores[:, n - 2, :]
            return work[:, slot_of(stage, name, n), :]

        CUT = LK - 2 * P
        S_OFF = BANK - CUT
        all_scores = lambda q: scores[0:QT, q, S_OFF:S_OFF + LK]
        hid_place = lambda stage: (work[0:RE, slot_of(stage, "hid"), 0:LQ] if stage == "tail"
                                   else scores[0:RE, 0, 0:LQ])
        assert 0 <= S_OFF < BANK
        acc = scores[:, 1, :].rearrange("p (i c) -> p i c", i=2)
        wT = scores[:, 0, :].rearrange("p (i c) -> p i c", i=WB)
        FIRST_W = 4

        def w_bank(c, k):
            if isinstance(c, int) and c == 0 and k < FIRST_W:
                return work[:, k // 2, (k % 2) * BANK:(k % 2 + 1) * BANK]
            return wT[:, k % WB, :]

        ident_ready = sem("ident_ready")
        consts_ready = sem("consts_ready")
        ar_loaded = sem("ar_loaded")
        raw_loaded = [sem(f"raw_loaded{c}") for c in range(CH)]
        x_first = [sem(f"x_first{c}") for c in range(CH)]
        xn_loaded = sem("xn_loaded")
        xres_loaded = sem("xres_loaded")
        filled = sem("filled")
        high_done = sem("high_done")
        drained = sem("drained")
        score_step = sem("score_step")
        scores_done = sem("scores_done")
        max_ready = sem("max_ready")
        exp_done = sem("exp_done")
        rinv_ready = sem("rinv_ready")
        val_high = sem("val_high")
        val_ready = sem("val_ready")
        val_used = sem("val_used")
        pv_done = sem("pv_done")
        ln1_first = [sem(f"ln1_first{i}") for i in range(NQ)]
        ln2_last = [sem(f"ln2_last{i}") for i in range(NQ)]
        x2_done = sem("x2_done")
        x2_stored = sem("x2_stored")
        stat1, aggr1, var1, rstd1, bias1 = (sem(f"ln1_{n}") for n in ("stats", "aggr", "var", "rstd", "bias"))
        stat2, aggr2, var2, rstd2, bias2 = (sem(f"ln2_{n}") for n in ("stats", "aggr", "var", "rstd", "bias"))
        ln1_done = sem("ln1_done")
        ln2_done = sem("ln2_done")
        xT_staged = sem("xT_staged")
        xT_stored = sem("xT_stored")
        gT_stored = sem("gT_stored")
        route = sem("route")
        rexp_done = sem("rexp_done")
        gated_done = sem("gated_done")

        piece_loaded = [sem(f"piece_loaded{i}") for i in range(RING)]
        w_filled = sem("w_filled")
        w_high = sem("w_high")
        w_ready = sem("w_ready")
        ax_loaded = sem("ax_loaded")
        ag_loaded = sem("ag_loaded")
        ax_high = sem("ax_high")
        ag_high = sem("ag_high")
        ax_low = sem("ax_low")
        ag_low = sem("ag_low")
        res_loaded = [sem(f"res_loaded{i}") for i in range(2)]
        bias_loaded = sem("bias_loaded")
        res_ready = sem("res_ready")
        tile_done = sem("tile_done")
        out_ready = sem("out_ready")
        out_stored = [sem(f"out_stored{i}") for i in range(2)]

        LOADS = [OT if p < BP else 1 for p in range(NP)]

        def piece_count(c, p):
            mine = [j for j in range(NP) if j % RING == p % RING]
            total = 16 * sum(LOADS[j] for j in mine)
            return c * total + 16 * sum(LOADS[j] for j in mine if j <= p)

        def load_piece(eng, c, p):
            s = p % RING
            if p >= BP:
                cols = slice((p - BP) * PK * P, (p - BP + 1) * PK * P)
                src = W[bass.ds(c * BANK, BANK), cols].rearrange("(o p) i -> p o i", p=P)
                eng.dma_start(piece[:, s, :, :], src).then_inc(piece_loaded[s], 16)
            else:
                for o in range(OT):
                    src = Bw[p * EP:(p + 1) * EP, bass.ds(c * BANK + o * P, P), :].rearrange("e p r -> p e r")
                    dst = piece[:, s, o, :].rearrange("p (e r) -> p e r", e=EP)
                    eng.dma_start(dst, src).then_inc(piece_loaded[s], 16)

        STATS_AT, SHIFT_AT, SPLIT_AT, LN2_LAST_AT, X2T_AT, HID_AT, HN_TAIL_AT = 2, 3, 3, 4, 8, 13, 15
        OVER_NT_AT = 14
        GT_TAIL_AT = 18
        FIRST_G_AT, FIRST_X_AT = 16, (21, 22, 23, 23)
        SECOND_G_AT, SECOND_X_AT = 5, (7, 9, 11, 12)

        block = stack.enter_context(nc.Block())

        @block.sync
        def _(sp):
            def load_raw(b, c):
                cols = slice(c * BANK, (c + 1) * BANK)
                sp.dma_start(raw[:, 0:FULL, cols],
                             ctx[b, 0:FULL * P, cols].rearrange("(t p) d -> p t d", p=P)).then_inc(raw_loaded[c], 16)
                sp.dma_start(raw[0:REST, FULL, cols], ctx[b, FULL * P:LK, cols]).then_inc(raw_loaded[c], 16)

            def one(b, stage):
                last = stage == "last"
                if not last:
                    if stage == "first":
                        sp.wait_ge(filled, job_no("pre", 0, "qT", NX - 1) + 1)
                    else:
                        sp.wait_ge(filled, job_no("mid", b, "ctxT", 0))
                    sp.dma_start(xn[:, :, :], x_v[b + 1]).then_inc(xn_loaded, 16)
                if stage != "first":
                    sp.wait_ge(filled, job_no(stage, b, "x2T", NX - 1) + 1)
                sp.dma_start(x2[:, :, :], x_v[b]).then_inc(xres_loaded, 16)
                for c in range(CH):
                    if not last:
                        sp.wait_ge(val_ready, b * (CH * NT) + (c + 1) * NT)
                        load_raw(b + 1, c)
                    if last and c == 0:
                        sp.wait_ge(filled, job_no(stage, b, "eT", NQ - 1) + 1)
                        sp.wait_ge(xT_stored, (NB - 2) * 16)
                        sp.wait_ge(gT_stored, (NB - 2) * 16)
                        load_tile(0, 0)
                    if stage != "first" and c == 0:
                        store_xT(b - 1)
                done = 0
                if last:
                    done = (CH - 1) * BANK
                    sp.wait_ge(x2_done, b * (NQ * CH) + NQ * (CH - 1))
                    sp.dma_start(x2_v[b][:, :, 0:done], x2[:, :, 0:done]).then_inc(x2_stored, 16)
                if stage != "first":
                    store_gT(b - 1, drained_gT=job_no(stage, b, "gT", NG - 1) + 1)
                sp.wait_ge(x2_done, (b + 1) * (NQ * CH))
                sp.dma_start(x2_v[b][:, :, done:D], x2[:, :, done:D]).then_inc(x2_stored, 16)

            def store_xT(b):
                sp.wait_ge(xT_staged, (b + 1) * NX)
                sp.dma_start(xT_d[:, :, bass.ds(b * LQ, LQ)], xT_st[:, :, :]).then_inc(xT_stored, 16)

            def store_gT(b, drained_gT):
                sp.wait_ge(drained, drained_gT)
                sp.dma_start(gT_d[:, :, bass.ds(b * LQ, LQ)], gT_st[:, :, :]).then_inc(gT_stored, 16)

            def load_tile(c, t):
                g = c * TT + t
                at_least(sp, ag_low, g)
                sp.dma_start(a_raw[:, 0:KB, :], gT_d[:, :, bass.ds(t * P, P)]).then_inc(ag_loaded, 16)
                at_least(sp, ax_low, g * XP)
                sp.dma_start(a_raw[:, KB:K, :], xT_d[:, :, bass.ds(t * P, P)]).then_inc(ax_loaded, 16)

            def load_res(c, t, par, half):
                at_least(sp, out_stored[par], half * 16)
                sp.dma_start(res[:, par, :], x2_d[bass.ds(t * P, P), bass.ds(c * BANK, BANK)]).then_inc(
                    res_loaded[par], 16)

            def load_bias(c):
                at_least(sp, res_ready, c * TT)
                sp.dma_start(bias_b[:, :], bias[bass.ds(c * BANK, BANK)].unsqueeze(0).to_broadcast([P, BANK])
                             ).then_inc(bias_loaded, 16)

            def next_piece(c, p):
                sp.wait_ge(w_filled, c * K + (p + 1) * PK)
                if p + RING < NP:
                    load_piece(sp, c, p + RING)
                else:
                    load_piece(sp, c + 1, p + RING - NP)

            def pair(c, i):
                for par in range(2):
                    load_tile(c, i * 2 + par)
                    load_res(c, i * 2 + par, par, c * (TT // 2) + i)

            def chunk(c, more):
                load_tile(c, 0)
                load_bias(c)
                load_res(c, 0, 0, c * (TT // 2))
                load_tile(c, 1)
                next_piece(c, 0)
                load_res(c, 1, 1, c * (TT // 2))
                for p in range(1, NP if more else NP - RING):
                    next_piece(c, p)
                with sp.Fori(1, TT // 2) as i:
                    pair(c, i)

            for c in range(CH):
                cols = slice(c * BANK, (c + 1) * BANK)
                sp.dma_start(xn[:, :, cols], x_v[0][:, :, cols]).then_inc(x_first[c], 16)
            sp.wait_ge(consts_ready, 1)
            for c in range(CH):
                load_raw(0, c)
            an = gated[0:RE, :, :].rearrange("p q g -> p (q g)")
            sp.dma_start(an[0:R, :], A).then_inc(ar_loaded, 16)
            sp.dma_start(an[R:RE, :], router).then_inc(ar_loaded, 16)
            one(0, "first")
            with sp.Fori(1, NB - 1) as b:
                one(b, "mid")
            one(NB - 1, "last")
            load_piece(sp, 0, RING - 1)
            next_piece(0, 0)
            load_bias(0)
            load_res(0, 0, 0, 0)
            load_res(0, 1, 1, 0)
            load_tile(0, 1)
            for p in range(1, NP - RING):
                next_piece(0, p)
            store_xT(NB - 1)
            for p in range(NP - RING, NP):
                next_piece(0, p)
            pair(0, 1)
            store_gT(NB - 1, drained_gT=job_no("tail", NB, "gT", NG - 1) + 1)
            sp.wait_ge(xT_stored, NB * 16)
            sp.wait_ge(gT_stored, NB * 16)
            with sp.Fori(2, TT // 2) as i:
                pair(0, i)
            with sp.Fori(1, NC - 1) as c:
                chunk(c, True)
            chunk(NC - 1, False)

        @block.tensor
        def _(pe):
            def take(no):
                at_least(pe, drained, no - 1)

            def transpose_block(stage, b, k):
                if k % (KD // CH) == 0:
                    pe.wait_ge(raw_loaded[k // (KD // CH)], b * 32 + 32)
                if stage == "first" and k < 2:
                    pe.wait_ge(drained, k + 1)
                else:
                    take(job_no(stage, b, "ctxT", k))
                slot = slot_of(stage, "ctxT", k)
                for t in range(NT):
                    rows = P if t < FULL else REST
                    last = pe.transpose(work[:, slot, t * P:t * P + rows],
                                        raw[0:rows, t, k * P:(k + 1) * P], ident[0:rows, 0:rows])
                last.then_inc(filled, 1)

            def scores_of(b, stage):
                job = lambda k: job_no(stage, b, "ctxT", k)

                def products(k, q):
                    for lo, hi in ((0, CUT), (CUT, LK)):
                        out = all_scores(q)[:, lo:hi]
                        qh = nT_h[:, k, q * QT:(q + 1) * QT]
                        ql = nT_l[:, k, q * QT:(q + 1) * QT]
                        ch = ctxT_h[:, k % CT, lo:hi]
                        cl = ctxT_l[:, k % CT, lo:hi]
                        pe.matmul(out, qh, ch, start=(k == 0), stop=False)
                        pe.matmul(out, qh, cl, start=False, stop=False)
                        last = pe.matmul(out, ql, ch, start=False, stop=(k == KD - 1))
                    return last

                if stage == "first":
                    transpose_block(stage, b, 0)
                    transpose_block(stage, b, 1)
                for k in range(KD - 2):
                    transpose_block(stage, b, k + 2)
                    if stage != "first" and k + 2 in X2T_AFTER:
                        x2T_of(stage, b, b - 1, x2, (X2T_AFTER.index(k + 2),))
                    pe.wait_ge(drained, job(k) + 1)
                    for q in reversed(range(NQ)):
                        if stage != "first" and k == 0:
                            pe.wait_ge(x2_done, b * (NQ * CH) - q * NQ)
                        last = products(k, q)
                    last.then_inc(score_step, 1)
                for q in range(NQ):
                    for k in (KD - 2, KD - 1):
                        pe.wait_ge(drained, job(k) + 1)
                        last = products(k, q)
                    last.then_inc(scores_done, 1)

            def transpose_rows(stage, b, name, src, n):
                if stage != "pre":
                    take(job_no(stage, b, name, n))
                for i in range(4):
                    k = 4 * n + i
                    for q in range(NQ):
                        at = (i // 2) * BANK + (i % 2) * LQ + q * QT
                        last = pe.transpose(place(stage, name, n)[:, at:at + QT],
                                            src[:, q, k * P:(k + 1) * P], ident[0:QT, 0:QT])
                last.then_inc(filled, 1)

            def transpose_ar(n):
                pe.wait_ge(ar_loaded, 32)
                take(job_no("first", 0, "arT", n))
                an = gated[0:RE, :, :].rearrange("p q g -> p (q g)")
                for i in range(8):
                    k = 8 * n + i
                    at = (i // 4) * BANK + (i % 4) * RE
                    last = pe.transpose(work[:, slot_of("first", "arT", n), at:at + RE],
                                        an[:, k * P:(k + 1) * P], ident[0:RE, 0:RE])
                last.then_inc(filled, 1)

            def hidden_of(stage, b, lo=0, hi=KD):
                if stage == "tail":
                    take(job_no(stage, b, "hid"))
                else:
                    pe.wait_ge(exp_done, b * NQ + 1)
                out = hid_place(stage)
                for k in range(lo, hi):
                    if k % 4 == 0:
                        pe.wait_ge(drained, job_no(stage, b, "x2T", k // 4) + 1)
                    pe.matmul(out, ar_h[:, k, :], nT_h[:, k, :], start=(k == 0), stop=False)
                    pe.matmul(out, ar_h[:, k, :], nT_l[:, k, :], start=False, stop=False)
                    last = pe.matmul(out, ar_l[:, k, :], nT_h[:, k, :], start=False, stop=(k == KD - 1))
                if hi == KD:
                    last.then_inc(filled, 1)

            def x2T_of(stage, b, of, src, groups=range(NX)):
                pe.wait_ge(ln2_done, (of + 1) * NQ)
                for n in groups:
                    transpose_rows(stage, b, "x2T", src, n)

            def hidden_back(stage, b):
                take(job_no(stage, b, "hN"))
                pe.wait_ge(drained, job_no(stage, b, "hid") + 1)
                slot = slot_of(stage, "hN")
                for q in range(NQ):
                    last = pe.transpose(work[0:QT, slot, q * RE:(q + 1) * RE],
                                        hT[:, q * QT:(q + 1) * QT], ident[0:RE, 0:RE])
                last.then_inc(filled, 1)

            def exps_T(stage, b):
                for q in range(NQ):
                    pe.wait_ge(exp_done, b * NQ + q + 1)
                    take(job_no(stage, b, "eT", q))
                    slot = slot_of(stage, "eT", q)
                    for t in range(NT):
                        at = (t // 3) * BANK + (t % 3) * QT
                        last = pe.transpose(work[:, slot, at:at + QT],
                                            prob[:, q, t * P:(t + 1) * P], ident[0:QT, 0:QT])
                    last.then_inc(filled, 1)

            def outputs_of(stage, b):
                pe.wait_ge(drained, job_no(stage, b, "eT", NQ - 1) + 1)
                for e in range(CH * NT):
                    c, t = e // NT, e % NT
                    if stage != "last" and e in NEXT_AT:
                        transpose_block("mid", b + 1, NEXT_AT.index(e))
                    if stage == "first" and e in GT_AT:
                        transpose_ar(GT_AT.index(e))
                    if stage != "first":
                        if e == HN_AT:
                            hidden_back(stage, b)
                        if e in GT_AT:
                            pe.wait_ge(gated_done, b * NQ)
                            transpose_rows(stage, b, "gT", gated, GT_AT.index(e))
                    if stage == "last" and e in FIRST_W_AT:
                        for k in range(2):
                            transpose_weights(0, 2 * FIRST_W_AT.index(e) + k)
                    if stage != "last" and e in QT_AT:
                        pe.wait_ge(ln1_done, b * NQ + NQ)
                        transpose_rows(stage, b, "qT", xn, QT_AT.index(e))
                    if t == 0 and c >= 2:
                        pe.wait_ge(x2_done, b * (NQ * CH) + NQ * (c - 1))
                    pe.wait_ge(val_ready, b * (CH * NT) + e + 1)
                    for q in range(NQ):
                        out = scores[0:QT, (c + 1) % 2, q * BANK:(q + 1) * BANK]
                        eh, el = eT_h[:, q, t, :], eT_l[:, q, t, :]
                        vh, vl = val_h[:, e % NR, :], val_l[:, e % NR, :]
                        pe.matmul(out, eh, vh, start=(t == 0), stop=False)
                        pe.matmul(out, eh, vl, start=False, stop=False)
                        last = pe.matmul(out, el, vh, start=False, stop=(t == NT - 1))
                    last.then_inc(val_used, 1)

            def one(b, stage):
                scores_of(b, stage)
                if stage != "first":
                    x2T_of(stage, b, b - 1, x2, (NX - 1,))
                    hidden_of(stage, b, 0, HID_EARLY)
                exps_T(stage, b)
                if stage != "first":
                    hidden_of(stage, b, HID_EARLY, KD)
                outputs_of(stage, b)

            def gated_tail():
                pe.wait_ge(gated_done, NB * NQ)
                for n in range(NG):
                    transpose_rows("tail", NB, "gT", gated, n)

            def transpose_weights(c, k):
                p, kk = k // PK, k % PK
                if kk == 0:
                    pe.wait_ge(piece_loaded[p % RING], piece_count(c, p))
                if isinstance(c, int) and c == 0 and k < FIRST_W:
                    pe.wait_ge(drained, job_no("last", NB - 1, "gT", k // 2) + 1)
                elif isinstance(c, int) and c == 0 and k < FIRST_W + WB:
                    pe.wait_ge(x2_done, NB * NQ * CH)
                else:
                    pe.wait_ge(w_ready, c * K + k - WB + 1)
                for o in range(OT):
                    last = pe.transpose(w_bank(c, k)[:, o * P:(o + 1) * P],
                                        piece[:, p % RING, o, kk * P:(kk + 1) * P], ident[:, :])
                last.then_inc(w_filled, 1)

            def start_tile(g):
                if isinstance(g, int) and g < 2:
                    pe.wait_ge(x2_done, (NB - 1) * (NQ * CH) + NQ * (CH - 1))
                else:
                    pe.wait_ge(out_ready, g - 1)
                pe.wait_ge(ag_low, g + 1)

            def block_products(g, k, par):
                if k >= KB and (k - KB) % 4 == 0:
                    pe.wait_ge(ax_low, g * XP + (k - KB) // 4 + 1)
                o = acc[:, par, :]
                ah, al = a_block(par, k)
                pe.matmul(o, ah, w_hl[:, k, 0, :], start=(k == 0), stop=False)
                pe.matmul(o, ah, w_hl[:, k, 1, :], start=False, stop=False)
                last = pe.matmul(o, al, w_hl[:, k, 0, :], start=False, stop=(k == K - 1))
                if k == K - 1:
                    last.then_inc(tile_done, 1)

            def tile(g, par):
                start_tile(g)
                for k in range(K):
                    block_products(g, k, par)

            def chunk(c, more, hooks):
                g0 = c * TT
                ahead = FIRST_W if isinstance(c, int) and c == 0 else WB
                start_tile(g0)
                for k in range(K):
                    if k in hooks:
                        hooks[k]()
                    if ahead <= k + WB < K:
                        transpose_weights(c, k + WB)
                    pe.wait_ge(w_ready, c * K + k + 1)
                    block_products(g0, k, 0)
                start_tile(g0 + 1)
                for k in range(K):
                    if K + k in hooks:
                        hooks[K + k]()
                    block_products(g0 + 1, k, 1)
                with pe.Fori(1, TT // 2 - 1) as i:
                    tile(g0 + i * 2, 0)
                    tile(g0 + i * 2 + 1, 1)
                tile(g0 + TT - 2, 0)
                start_tile(g0 + TT - 1)
                for k in range(K):
                    block_products(g0 + TT - 1, k, 1)
                    if more and k in (12, 14):
                        transpose_weights(c + 1, (k - 12) // 2)

            pe.wait_ge(ident_ready, 2)
            for n in range(NX):
                for q in range(NQ):
                    pe.wait_ge(ln1_first[q], n + 1)
                transpose_rows("pre", 0, "qT", xn, n)
            one(0, "first")
            with pe.Fori(1, NB - 1) as b:
                one(b, "mid")
            one(NB - 1, "last")
            def x2T_last(n):
                for q in range(NQ):
                    pe.wait_ge(ln2_last[q], n + 1)
                transpose_rows("tail", NB, "x2T", x2, n)

            hooks = {
                HID_AT: lambda: hidden_of("tail", NB),
                HN_TAIL_AT: lambda: hidden_back("tail", NB),
                K + GT_TAIL_AT: gated_tail,
            }
            for n in range(NX):
                hooks[X2T_AT + n] = lambda n=n: x2T_last(n)
            chunk(0, True, hooks)
            with pe.Fori(1, NC - 1) as c:
                chunk(c, True, {})
            chunk(NC - 1, False, {})

        @block.scalar
        def _(act):
            def high(stage, b, name, n, out, cols, width):
                act.wait_ge(filled, job_no(stage, b, name, n) + 1)
                src = place(stage, name, n).rearrange("p (k c) -> p k c", k=cols)[:, :, 0:width]
                act.activation(out, src, ACT.Copy).then_inc(high_done, 1)

            def ctx_high(stage, b, k):
                if k >= CT:
                    act.wait_ge(score_step, b * (KD - 2) + k - CT + 1)
                act.wait_ge(filled, job_no(stage, b, "ctxT", k) + 1)
                act.activation(ctxT_h[:, k % CT, :], work[:, slot_of(stage, "ctxT", k), 0:LK],
                               ACT.Copy).then_inc(high_done, 1)

            def four_blocks(tile, n):
                return tile[:, 4 * n:4 * n + 4, :].rearrange("p (k i) c -> p k (i c)", k=2)

            def eight_blocks(tile, n):
                return tile[:, 8 * n:8 * n + 8, :].rearrange("p (k i) c -> p k (i c)", k=2)

            def quarter(tile, i, rstd, bias, sem_done):
                cols = slice(i * BANK, (i + 1) * BANK)
                act.activation(tile[:, 0, cols], tile[:, 0, cols], ACT.Identity, bias=bias[:, 0:1],
                               scale=rstd[:, 0:1]).then_inc(sem_done, 1)

            def normalise(out, tile, q, rstd, bias, sem_done):
                act.activation(out[:, q, :], tile[:, q, :], ACT.Identity, bias=bias[:, q:q + 1],
                               scale=rstd[:, q:q + 1]).then_inc(sem_done, 1)

            def value_high(b, e):
                at_least(act, val_used, b * (CH * NT) + e - NR + 1)
                c, t = e // NT, e % NT
                act.activation(val_h[:, e % NR, :], raw[:, t, c * BANK:(c + 1) * BANK],
                               ACT.Copy).then_inc(val_high, 1)

            def exponentials(b, q):
                act.wait_ge(max_ready, b * NQ + q + 1)
                act.activation(prob[:, q, 0:LK], all_scores(q), ACT.Exp, bias=nmax[:, q:q + 1],
                               scale=1.0, accum_out=rsum[:, q:q + 1]).then_inc(exp_done, 1)

            def routing_exp(of):
                act.wait_ge(route, of * ROUTE + 2)
                act.activation(t16[1][:, :, :], t16[0][:, :, :], ACT.Exp).then_inc(rexp_done, 1)

            def one(b, stage):
                for k in range(0 if stage == "first" else 2, KD):
                    ctx_high(stage, b, k)
                    if stage != "first" and k in (7, 9):
                        if k == 7:
                            act.wait_ge(bias2, b)
                            act.wait_ge(x2_stored, b * 16)
                        normalise(x2, x2, (k - 7) // 2, rs2, nb2, ln2_done)
                    if stage != "first" and k in X2T_AFTER:
                        n = X2T_AFTER.index(k)
                        high(stage, b, "x2T", n, four_blocks(nT_h, n), 2, 2 * LQ)
                    if k in (5, 8, 10, 11):
                        value_high(b, (5, 8, 10, 11).index(k))
                exponentials(b, 0)
                if stage != "first":
                    high(stage, b, "x2T", NX - 1, four_blocks(nT_h, NX - 1), 2, 2 * LQ)
                exponentials(b, 1)
                for q in range(NQ):
                    high(stage, b, "eT", q, eT_h[:, q, :, :].rearrange("p (k i) c -> p k (i c)", k=2), 2, 3 * QT)
                if stage == "last":
                    for p in range(RING - 1):
                        load_piece(act, 0, p)
                for e in range(NR, CH * NT):
                    value_high(b, e)
                    if stage == "last" and e == SPLIT_G_AT:
                        split_g(0, 0)
                    if stage != "last" and e in LN1_AT:
                        if e == LN1_AT[0]:
                            act.wait_ge(bias1, b + 2)
                        normalise(xn, xn, LN1_AT.index(e), rs1, nb1, ln1_done)
                    if stage != "first" and e == ROUTE_EXP_AT:
                        routing_exp(b - 1)
                    if stage != "last" and e - 3 in QT_AT:
                        n = QT_AT.index(e - 3)
                        if stage == "mid" and n == 0:
                            act.wait_ge(xT_staged, b * NX)
                        high(stage, b, "qT", n, four_blocks(nT_h, n), 2, 2 * LQ)
                    if stage == "first" and e - 3 in GT_AT:
                        n = GT_AT.index(e - 3)
                        high(stage, b, "arT", n, eight_blocks(ar_h, n), 2, 4 * RE)
                if stage != "last":
                    for k in range(2):
                        ctx_high("mid", b + 1, k)

            def weight_high(c, k):
                act.wait_ge(w_filled, c * K + k + 1)
                act.activation(w_hl[:, k, 0, :], w_bank(c, k), ACT.Copy).then_inc(w_high, 1)

            def split_g(g, par):
                act.wait_ge(ag_loaded, g * 16 + 16)
                act.activation(ag_h[par][:, :, :], a_raw[:, 0:KB, :], ACT.Copy).then_inc(ag_high, 1)

            def split_x(g, par, parts=range(XP)):
                act.wait_ge(ax_loaded, g * 16 + 16)
                for i in parts:
                    part = slice(4 * i, 4 * i + 4)
                    act.activation(ax_h[par][:, part, :], a_raw[:, KB:K, :][:, part, :],
                                   ACT.Copy).then_inc(ax_high, 1)

            def split_high(g, par):
                if not (isinstance(g, int) and g < 2):
                    act.wait_ge(tile_done, g - 1)
                split_g(g, par)
                split_x(g, par)

            def store(c, t, par):
                act.wait_ge(out_ready, c * TT + t + 1)
                act.dma_start(out[bass.ds(t * P, P), bass.ds(c * BANK, BANK)], res[:, par, :]).then_inc(
                    out_stored[par], 16)

            def store_last(c):
                store(c - 1, TT - 1, 1)

            def chunk(c, more, hooks):
                g0 = c * TT
                ahead = FIRST_W if isinstance(c, int) and c == 0 else WB
                for k in range(K):
                    if k in hooks:
                        hooks[k]()
                    if ahead <= k + WB < K:
                        weight_high(c, k + WB)
                if K in hooks:
                    hooks[K]()
                store(c, 0, 0)
                split_high(g0 + 2, 0)
                store(c, 1, 1)
                with act.Fori(1, TT // 2 - 1) as i:
                    split_high(g0 + i * 2 + 1, 1)
                    store(c, i * 2, 0)
                    split_high(g0 + i * 2 + 2, 0)
                    store(c, i * 2 + 1, 1)
                split_high(g0 + TT - 1, 1)
                store(c, TT - 2, 0)
                if more:
                    split_high(g0 + TT, 0)
                    weight_high(c + 1, 0)
                    weight_high(c + 1, 1)

            for n in range(NX):
                high("pre", 0, "qT", n, four_blocks(nT_h, n), 2, 2 * LQ)
            one(0, "first")
            with act.Fori(1, NB - 1) as b:
                one(b, "mid")
            one(NB - 1, "last")
            def normalise_last(i):
                if i == 0:
                    act.wait_ge(bias2, NB)
                    act.wait_ge(x2_stored, (NB + 1) * 16)
                quarter(x2, i, rs2, nb2, ln2_last[0])

            def x2T_last(n):
                high("tail", NB, "x2T", n, four_blocks(nT_h, n), 2, 2 * LQ)

            def over_nT():
                act.wait_ge(xT_staged, NB * NX)

            def first_x(parts):
                act.wait_ge(xT_stored, NB * 16)
                split_x(1, 1, parts)

            def hooks_of(c):
                def second_g():
                    act.wait_ge(tile_done, c * TT)
                    split_g(c * TT + 1, 1)
                hooks = {2: lambda: store_last(c), SECOND_G_AT: second_g}
                for i, at in enumerate(SECOND_X_AT):
                    hooks[at] = lambda i=i: split_x(c * TT + 1, 1, (i,))
                return hooks

            act.wait_ge(val_ready, NB * CH * NT)
            for k in range(FIRST_W):
                weight_high(0, k)
            act.wait_ge(val_used, NB * CH * NT)
            split_x(0, 0)
            hooks = {OVER_NT_AT: over_nT, K: lambda: routing_exp(NB - 1), FIRST_G_AT: lambda: split_g(1, 1)}
            for i in range(CH):
                hooks[LN2_LAST_AT + i] = lambda i=i: normalise_last(i)
            for n in range(NX):
                hooks[X2T_AT + n] = lambda n=n: x2T_last(n)
            for at in FIRST_X_AT:
                hooks[at] = lambda at=at: first_x([i for i in range(XP) if FIRST_X_AT[i] == at])
            chunk(0, True, hooks)
            with act.Fori(1, NC - 1) as c:
                chunk(c, True, hooks_of(c))
            chunk(NC - 1, False, hooks_of(NC - 1))
            store(NC - 1, TT - 1, 1)
            for par in range(2):
                act.wait_ge(out_stored[par], NC * (TT // 2) * 16)

        @block.vector
        def _(dve):
            def low(stage, b, name, n, high_part, low_part, cols, width):
                dve.wait_ge(high_done, act_no(stage, b, name, n) + 1)
                src = place(stage, name, n).rearrange("p (k c) -> p k c", k=cols)[:, :, 0:width]
                dve.tensor_tensor(low_part, src, as_f32(high_part), ALU.subtract).then_inc(drained, 1)

            def ctx_low(stage, b, k):
                dve.wait_ge(high_done, act_no(stage, b, "ctxT", k) + 1)
                dve.tensor_tensor(ctxT_l[:, k % CT, :], work[:, slot_of(stage, "ctxT", k), 0:LK],
                                  as_f32(ctxT_h[:, k % CT, :]), ALU.subtract).then_inc(drained, 1)

            def four_blocks(tile, n):
                return tile[:, 4 * n:4 * n + 4, :].rearrange("p (k i) c -> p k (i c)", k=2)

            def eight_blocks(tile, n):
                return tile[:, 8 * n:8 * n + 8, :].rearrange("p (k i) c -> p k (i c)", k=2)

            def value_low(b, e):
                c, t = e // NT, e % NT
                dve.wait_ge(val_high, b * (CH * NT) + e + 1)
                dve.tensor_tensor(val_l[:, e % NR, :], raw[:, t, c * BANK:(c + 1) * BANK],
                                  as_f32(val_h[:, e % NR, :]), ALU.subtract).then_inc(val_ready, 1)

            def stats(tile, st, sem_stat, i):
                q, c = i // CH, i % CH
                dve.bn_stats(st[:, q, c, :], tile[:, q, c * BANK:(c + 1) * BANK]).then_inc(sem_stat, 1)

            def aggregate(st, mv, sem_aggr):
                for q in range(NQ):
                    dve.bn_aggr(mv[:, q, :], st[:, q, :, :].rearrange("p c s -> p (c s)")).then_inc(sem_aggr, 1)

            def variance(mv, ve, sem_aggr, sem_var, n):
                dve.wait_ge(sem_aggr, n * NQ + NQ)
                dve.tensor_scalar(ve[:, :], mv[:, :, 1], EPS, None, ALU.add).then_inc(sem_var, 1)

            def shift(mv, rs, nb, sem_rstd, sem_bias, n):
                dve.wait_ge(sem_rstd, n + 1)
                dve.scalar_tensor_tensor(nb[:, :], mv[:, :, 0], -1.0, rs[:, :], ALU.mult,
                                         ALU.mult).then_inc(sem_bias, 1)

            def row_max(b):
                for q in range(NQ):
                    dve.wait_ge(scores_done, b * NQ + q + 1)
                    dve.reduce_max(nmax[:, q:q + 1], all_scores(q), AX.X,
                                   negate=True).then_inc(max_ready, 1)

            def residual(b, c):
                if c == 0:
                    dve.wait_ge(exp_done, b * NQ + NQ)
                    dve.reciprocal(rinv[:, :], rsum[:, :]).then_inc(rinv_ready, 1)
                    dve.wait_ge(xres_loaded, b * 16 + 16)
                    dve.wait_ge(rinv_ready, b + 1)
                dve.wait_ge(val_used, b * (CH * NT) + (c + 1) * NT)
                for q in range(NQ):
                    cols = slice(c * BANK, (c + 1) * BANK)
                    dve.scalar_tensor_tensor(x2[:, q, cols], scores[0:QT, (c + 1) % 2, q * BANK:(q + 1) * BANK],
                                             rinv[:, q:q + 1], x2[:, q, cols], ALU.mult,
                                             ALU.add).then_inc(x2_done, 1)

            def hidden_out(stage, b):
                dve.wait_ge(filled, job_no(stage, b, "hid") + 1)
                dve.tensor_copy(hT[:, :], hid_place(stage)).then_inc(drained, 1)

            def hidden_back(stage, b):
                dve.wait_ge(filled, job_no(stage, b, "hN") + 1)
                dve.tensor_copy(hn[:, :, :].rearrange("p q r -> p (q r)"),
                                work[0:QT, slot_of(stage, "hN"), 0:NQ * RE]).then_inc(drained, 1)

            def wide(v):
                return v.unsqueeze(2).to_broadcast([QT, NQ, E])

            rank_w = rank[:, :].unsqueeze(1).to_broadcast([QT, NQ, E])

            def route_steps(stage, b, of):
                logits = hn[:, :, R:RE]
                z, ez, p, eq1, key1, one1, p_rest, eq2, key2, one2 = (t[:, :, :] for t in t16)
                lmax, s, rs, m1, k1, m2, k2, den, rden = (t[:, :] for t in t1)
                v = dve
                return [
                    lambda: v.reduce_max(lmax, logits, AX.X),
                    lambda: v.tensor_tensor(z, logits, wide(lmax), ALU.subtract),
                    lambda: v.reduce_sum(s, ez, AX.X),
                    lambda: v.reciprocal(rs, s),
                    lambda: v.tensor_tensor(p, ez, wide(rs), ALU.mult),
                    lambda: v.reduce_max(m1, p, AX.X),
                    lambda: v.tensor_tensor(eq1, p, wide(m1), ALU.is_equal),
                    lambda: v.tensor_tensor(key1, eq1, rank_w, ALU.mult),
                    lambda: v.reduce_max(k1, key1, AX.X),
                    lambda: v.tensor_tensor(one1, key1, wide(k1), ALU.is_equal),
                    lambda: v.scalar_tensor_tensor(p_rest, one1, -2.0, p, ALU.mult, ALU.add),
                    lambda: v.reduce_max(m2, p_rest, AX.X),
                    lambda: v.tensor_tensor(eq2, p_rest, wide(m2), ALU.is_equal),
                    lambda: v.tensor_tensor(key2, eq2, rank_w, ALU.mult),
                    lambda: v.reduce_max(k2, key2, AX.X),
                    lambda: v.tensor_tensor(one2, key2, wide(k2), ALU.is_equal),
                    lambda: v.tensor_tensor(one1, one1, one2, ALU.add),
                    lambda: v.tensor_tensor(den, m1, m2, ALU.add),
                    lambda: v.tensor_scalar(den, den, TOP_EPS, 1.0 / SCALING, ALU.add, ALU.mult),
                    lambda: v.reciprocal(rden, den),
                    lambda: v.tensor_tensor(z, one1, p, ALU.mult),
                    lambda: v.tensor_tensor(ez, z, wide(rden), ALU.mult),
                ]

            def run_route(stage, b, of, lo, hi):
                steps = route_steps(stage, b, of)
                assert len(steps) == ROUTE
                for n in range(lo, hi):
                    if n == 0:
                        dve.wait_ge(drained, job_no(stage, b, "hN") + 1)
                    else:
                        dve.wait_ge(route, of * ROUTE + n)
                    if n == 2:
                        dve.wait_ge(rexp_done, of + 1)
                    steps[n]().then_inc(route, 1)

            def gated_T(stage, b, of, n):
                if n == 0:
                    at_least(dve, gT_stored, of * 16)
                dve.wait_ge(filled, job_no(stage, b, "gT", n) + 1)
                src = work[:, slot_of(stage, "gT", n), :].rearrange("p (k c) -> p k c", k=2)[:, :, 0:2 * LQ]
                dve.tensor_copy(four_blocks(gT_st, n), src).then_inc(drained, 1)

            def one(b, stage):
                old, new = stage != "first", stage != "last"
                x2T_low = lambda n: low(stage, b, "x2T", n, four_blocks(nT_h, n), four_blocks(nT_l, n), 2, 2 * LQ)
                for k in range(KD):
                    if k >= 2 or stage == "first":
                        ctx_low(stage, b, k)
                    if old and k < 4:
                        if k == 0:
                            dve.wait_ge(x2_done, b * (NQ * CH))
                        stats(x2, st2, stat2, 2 * k)
                        stats(x2, st2, stat2, 2 * k + 1)
                        if k == 3:
                            dve.wait_ge(stat2, b * (NQ * CH))
                    if old and k == 4:
                        aggregate(st2, mv2, aggr2)
                        variance(mv2, ve2, aggr2, var2, b - 1)
                    if old and k == 5:
                        shift(mv2, rs2, nb2, rstd2, bias2, b - 1)
                    if new and 6 <= k < 10:
                        if k == 6:
                            dve.wait_ge(xn_loaded, b * 16 + 16)
                        stats(xn, st1, stat1, 2 * (k - 6))
                        stats(xn, st1, stat1, 2 * (k - 6) + 1)
                        if k == 9:
                            dve.wait_ge(stat1, b * (NQ * CH) + 2 * NQ * CH)
                    if new and k == 10:
                        aggregate(st1, mv1, aggr1)
                        variance(mv1, ve1, aggr1, var1, b + 1)
                    if new and k == 11:
                        shift(mv1, rs1, nb1, rstd1, bias1, b + 1)
                    if old and k in X2T_AFTER:
                        x2T_low(X2T_AFTER.index(k))
                    if k in (11, 12, 13, 14):
                        value_low(b, k - 11)
                row_max(b)
                if old:
                    x2T_low(NX - 1)
                for q in range(NQ):
                    three = lambda tile: tile[:, q, :, :].rearrange("p (k i) c -> p k (i c)", k=2)
                    low(stage, b, "eT", q, three(eT_h), three(eT_l), 2, 3 * QT)
                if old:
                    hidden_out(stage, b)
                for e in range(NR, CH * NT):
                    value_low(b, e)
                    c, t = e // NT, e % NT
                    if old and e == HN_AT + 3:
                        hidden_back(stage, b)
                    if old and e in ROUTE_AT:
                        run_route(stage, b, b - 1, *ROUTE_AT[e])
                    if new and e - 3 in QT_AT:
                        n = QT_AT.index(e - 3)
                        low(stage, b, "qT", n, four_blocks(nT_h, n), four_blocks(nT_l, n), 2, 2 * LQ)
                    if old and e - 3 in GT_AT:
                        gated_T(stage, b, b - 1, GT_AT.index(e - 3))
                    if stage == "first" and e - 3 in GT_AT:
                        n = GT_AT.index(e - 3)
                        low(stage, b, "arT", n, eight_blocks(ar_h, n), eight_blocks(ar_l, n), 2, 4 * RE)
                    if c >= 1 and t == 3:
                        residual(b, c - 1)
                    if not new and c >= 1 and t in (4, 5):
                        if t == 4:
                            dve.wait_ge(x2_done, b * (NQ * CH) + c * NQ)
                        stats(x2, st2, stat2, (t - 4) * CH + c - 1)
                if not new:
                    for k in range(FIRST_W):
                        weight_low(0, k)
                else:
                    for k in range(2):
                        ctx_low("mid", b + 1, k)
                residual(b, CH - 1)

            def weight_low(c, k):
                dve.wait_ge(w_high, c * K + k + 1)
                dve.tensor_tensor(w_hl[:, k, 1, :], w_bank(c, k), as_f32(w_hl[:, k, 0, :]),
                                  ALU.subtract).then_inc(w_ready, 1)

            def split_low(g, par, parts=range(XP)):
                for i in parts:
                    dve.wait_ge(ax_high, g * XP + i + 1)
                    part = slice(4 * i, 4 * i + 4)
                    dve.tensor_tensor(ax_l[par][:, part, :], a_raw[:, KB:K, :][:, part, :],
                                      as_f32(ax_h[par][:, part, :]), ALU.subtract).then_inc(ax_low, 1)

            def finish(g, par):
                dve.wait_ge(res_ready, g + 1)
                dve.wait_ge(tile_done, g + 1)
                dve.tensor_tensor(res[:, par, :], acc[:, par, :], res[:, par, :], ALU.add).then_inc(out_ready, 1)

            def chunk(c, more, hooks):
                g0 = c * TT
                ahead = FIRST_W if isinstance(c, int) and c == 0 else WB
                for k in range(K):
                    if k in hooks:
                        hooks[k]()
                    if ahead <= k + WB < K:
                        weight_low(c, k + WB)
                if K in hooks:
                    hooks[K]()
                finish(g0, 0)
                split_low(g0 + 2, 0)
                if K + 1 in hooks:
                    hooks[K + 1]()
                finish(g0 + 1, 1)
                with dve.Fori(1, TT // 2 - 1) as i:
                    split_low(g0 + i * 2 + 1, 1)
                    finish(g0 + i * 2, 0)
                    split_low(g0 + i * 2 + 2, 0)
                    finish(g0 + i * 2 + 1, 1)
                split_low(g0 + TT - 1, 1)
                finish(g0 + TT - 2, 0)
                if more:
                    split_low(g0 + TT, 0)
                    weight_low(c + 1, 0)
                    weight_low(c + 1, 1)

            dve.memset(raw[96:P, FULL, :], 0.0).then_inc(consts_ready, 1)
            dve.memset(prob[:, :, LK:NT * P], 0.0).then_inc(consts_ready, 1)
            for e in range(E):
                dve.memset(rank[:, e:e + 1], float(E - e)).then_inc(consts_ready, 1)
            for c in range(CH):
                dve.wait_ge(x_first[c], 16)
                for q in range(NQ):
                    stats(xn, st1, stat1, q * CH + c)
            dve.wait_ge(stat1, NQ * CH)
            aggregate(st1, mv1, aggr1)
            variance(mv1, ve1, aggr1, var1, 0)
            shift(mv1, rs1, nb1, rstd1, bias1, 0)
            dve.wait_ge(bias1, 1)
            for i in range(CH):
                cols = slice(i * BANK, (i + 1) * BANK)
                dve.tensor_scalar(xn[:, 0, cols], xn[:, 0, cols], rs1[:, 0:1], nb1[:, 0:1], ALU.mult,
                                  ALU.add).then_inc(ln1_first[0], 1)
            for n in range(NX):
                low("pre", 0, "qT", n, four_blocks(nT_h, n), four_blocks(nT_l, n), 2, 2 * LQ)
            dve.wait_ge(consts_ready, 2 + E)
            one(0, "first")
            with dve.Fori(1, NB - 1) as b:
                one(b, "mid")
            one(NB - 1, "last")
            def last_stats():
                dve.wait_ge(x2_done, NB * NQ * CH)
                for q in range(NQ):
                    stats(x2, st2, stat2, q * CH + CH - 1)
                dve.wait_ge(stat2, NB * NQ * CH)
                aggregate(st2, mv2, aggr2)
                variance(mv2, ve2, aggr2, var2, NB - 1)

            def x2T_last(n):
                low("tail", NB, "x2T", n, four_blocks(nT_h, n), four_blocks(nT_l, n), 2, 2 * LQ)

            hooks = {
                STATS_AT: last_stats,
                SHIFT_AT: lambda: shift(mv2, rs2, nb2, rstd2, bias2, NB - 1),
                HID_AT: lambda: hidden_out("tail", NB),
                HN_TAIL_AT: lambda: hidden_back("tail", NB),
                K: lambda: run_route("tail", NB, NB - 1, 0, ROUTE),
                K + 1: lambda: [gated_T("tail", NB, NB - 1, n) for n in range(NG)],
            }
            for n in range(NX):
                hooks[X2T_AT + n] = lambda n=n: x2T_last(n)
            for i in range(XP):
                def part(i=i, before=hooks.get(SPLIT_AT + i)):
                    if before:
                        before()
                    split_low(0, 0, (i,))
                hooks[SPLIT_AT + i] = part
            for at in FIRST_X_AT:
                hooks[at] = lambda at=at: split_low(1, 1, [i for i in range(XP) if FIRST_X_AT[i] == at])
            chunk(0, True, hooks)

            def hooks_of(c):
                hooks = {0: lambda: finish(c * TT - 1, 1)}
                for i, at in enumerate(SECOND_X_AT):
                    hooks[at] = lambda i=i: split_low(c * TT + 1, 1, (i,))
                return hooks

            with dve.Fori(1, NC - 1) as c:
                chunk(c, True, hooks_of(c))
            chunk(NC - 1, False, hooks_of(NC - 1))
            finish(NC * TT - 1, 1)

        @block.gpsimd
        def _(pool):
            def reciprocal_root(ve, rs, sem_var, sem_rstd, n):
                pool.wait_ge(sem_var, n + 1)
                pool.tensor_tensor(rs[:, :], ve[:, :], mhalf[:, :], ALU.pow).then_inc(sem_rstd, 1)

            def normalise_second(tile, rstd, bias, sem_done):
                for i in range(CH):
                    cols = slice(i * BANK, (i + 1) * BANK)
                    pool.tensor_scalar(tile[:, 1, cols], tile[:, 1, cols], rstd[:, 1:2], bias[:, 1:2], ALU.mult,
                                       ALU.add).then_inc(sem_done, 1)

            def stage_xT(stage, b, of):
                if not (isinstance(of, int) and of == 0):
                    at_least(pool, xT_stored, of * 16)
                for n in range(NX):
                    pool.wait_ge(drained, job_no(stage, b, "x2T", n) + 1)
                    cut = slice(4 * n, 4 * n + 4)
                    pool.tensor_tensor(xT_st[:, cut, :], as_f32(nT_h[:, cut, :]), as_f32(nT_l[:, cut, :]),
                                       ALU.add).then_inc(xT_staged, 1)

            def gate(of):
                pool.wait_ge(route, of * ROUTE + ROUTE)
                for q in range(NQ):
                    pool.tensor_tensor(gated[:, q, :].rearrange("p (e r) -> p e r", e=E),
                                       t16[1][:, q, :].unsqueeze(2).to_broadcast([QT, E, R]),
                                       hn[:, q, 0:R].unsqueeze(1).to_broadcast([QT, E, R]),
                                       ALU.mult).then_inc(gated_done, 1)

            def split_low(g, par):
                pool.wait_ge(ag_high, g + 1)
                pool.tensor_tensor(ag_l[par][:, :, :], a_raw[:, 0:KB, :], as_f32(ag_h[par][:, :, :]),
                                   ALU.subtract).then_inc(ag_low, 1)

            def add_bias(c, g, par, half):
                pool.wait_ge(bias_loaded, c * 16 + 16)
                pool.wait_ge(res_loaded[par], half * 16 + 16)
                pool.tensor_tensor(res[:, par, :], res[:, par, :], bias_b[:, :], ALU.add).then_inc(res_ready, 1)

            def tile(c, g, par, half):
                split_low(g, par)
                add_bias(c, g, par, half)

            def pair(c, i):
                for par in range(2):
                    tile(c, c * TT + i * 2 + par, par, c * (TT // 2) + i)

            build_identity(pool, ident, ident_ready)
            pool.memset(mhalf[:, :], -0.5).then_inc(ident_ready, 1)
            pool.wait_ge(ident_ready, 3)
            reciprocal_root(ve1, rs1, var1, rstd1, 0)
            pool.wait_ge(bias1, 1)
            normalise_second(xn, rs1, nb1, ln1_first[1])
            reciprocal_root(ve1, rs1, var1, rstd1, 1)
            with pool.Fori(1, NB - 1) as b:
                reciprocal_root(ve2, rs2, var2, rstd2, b - 1)
                reciprocal_root(ve1, rs1, var1, rstd1, b + 1)
                stage_xT("mid", b, b - 1)
                gate(b - 1)
            reciprocal_root(ve2, rs2, var2, rstd2, NB - 2)
            stage_xT("last", NB - 1, NB - 2)
            gate(NB - 2)
            split_low(0, 0)
            reciprocal_root(ve2, rs2, var2, rstd2, NB - 1)
            pool.wait_ge(x2_stored, (NB + 1) * 16)
            pool.wait_ge(bias2, NB)
            normalise_second(x2, rs2, nb2, ln2_last[1])
            stage_xT("tail", NB, NB - 1)
            add_bias(0, 0, 0, 0)
            split_low(1, 1)
            gate(NB - 1)
            add_bias(0, 1, 1, 0)
            with pool.Fori(1, TT // 2) as i:
                pair(0, i)
            with pool.Fori(1, NC) as c:
                with pool.Fori(0, TT // 2) as i:
                    pair(c, i)


_INS = ["x", "ctx_4096", "L0_ffn_base_w", "L0_ffn_base_b", "L0_ffn_A", "L0_ffn_B", "L0_ffn_router_w"]
_OUTS = [((8, 224, 2048), "float32")]


def kernel(**inputs):
    import numpy as _np
    import concourse.bacc as _bacc
    from concourse import mybir as _mybir
    from concourse.bass_utils import run_bass_kernel_spmd as _run

    nc = _bacc.Bacc("TRN2", target_bir_lowering=False, num_devices=1)
    arrays, args = {}, []
    for name in _INS:
        a = _np.ascontiguousarray(inputs[name])
        arrays[f"in_{name}_dram"] = a
        args.append(nc.dram_tensor(f"in_{name}_dram", a.shape, _mybir.dt.from_np(a.dtype), kind="ExternalInput").ap())
    for i, (shape, dtype) in enumerate(_OUTS):
        dt = _mybir.dt.from_np(_np.dtype(dtype))
        args.append(nc.dram_tensor(f"out_{i}_dram", shape, dt, kind="ExternalOutput").ap())
    xattn_ffn_kernel(nc, *args)
    r = _run(nc, [arrays], core_ids=[0])
    got = tuple(r.results[0][f"out_{i}_dram"] for i in range(len(_OUTS)))
    return got[0]
```
